# Optimizing a Trainium2 kernel written in Bass

```python
import numpy as np
import jax
import jax.numpy as jnp

def _softmax(x, axis=-1):
    return jax.nn.softmax(x, axis=axis)

def _gelu(x):
    return jax.nn.gelu(x, approximate=True)

def _silu(x):
    return jax.nn.silu(x)

def _sigmoid(x):
    return jax.nn.sigmoid(x)

def _layernorm(x, axis=-1, eps=1e-05):
    m = jnp.mean(x, axis=axis, keepdims=True)
    v = jnp.var(x, axis=axis, keepdims=True)
    return (x - m) / jnp.sqrt(v + eps)

def _scatter_add(tgt, idx, src, axis=0):
    return tgt.at[idx].add(src)

def _segment_sum(src, seg, n):
    return jax.ops.segment_sum(src, seg, n)
kernel_name = 'mk_audio_tower_d1_tok_audfeat512_r4_58e2a1'

def setup_inputs(seed: int=0):
    np.random.seed(seed)
    _w = jnp.asarray

    def _rec_inputs():
        import jax
        import jax.numpy as jnp
        _rk = jax.random.key(seed)
        x = -0.000292821 + 1.00034 * jax.random.normal(jax.random.fold_in(_rk, 1), (64, 750, 2), jnp.float32)
        return x
    x = _rec_inputs()

    def _L0_tok_setup():
        import jax, jax.numpy as jnp
        import numpy as np
        PATCH_LENGTH = 128
        PATCH_STRIDE = 64
        MODEL_DIM = 128
        LN_EPS = 0.001
        key = jax.random.key(seed)
        k1, k2 = jax.random.split(key)
        B, T, C = (64, 8192, 2)
        x = jax.random.normal(k1, (B, T, C), dtype=jnp.float32)
        in_dim = PATCH_LENGTH * C
        W = jax.random.normal(k2, (in_dim, MODEL_DIM), dtype=jnp.float32) / np.sqrt(in_dim)
        b = jnp.zeros((MODEL_DIM,), dtype=jnp.float32)
        gamma = jnp.ones((MODEL_DIM,), dtype=jnp.float32)
        beta = jnp.zeros((MODEL_DIM,), dtype=jnp.float32)
        return {'x': x, 'W': W, 'b': b, 'gamma': gamma, 'beta': beta}
    _L0_tok_all = _L0_tok_setup()
    _L0_tok_in = {k: v for k, v in _L0_tok_all.items() if k in ('W', 'b', 'gamma', 'beta')}
    del _L0_tok_all

    def _L0_attn_setup():
        import jax, jax.numpy as jnp
        import numpy as np
        D_MODEL = 128
        N_HEADS = 8
        DH = D_MODEL // N_HEADS
        Q_PROJ = D_MODEL // 2
        KV_PROJ = 2 * D_MODEL // 3
        ROPE_DIM = D_MODEL // 8
        R = ROPE_DIM // N_HEADS
        THETA = 10000.0
        EPS = 1e-05
        B, S = (2, 512)

        def layernorm(x, g, b):
            m = jnp.mean(x, axis=-1, keepdims=True)
            v = jnp.var(x, axis=-1, keepdims=True)
            return (x - m) * jax.lax.rsqrt(v + EPS) * g + b

        def rope_cos_sin(seq_len, dtype):
            inv_freq = THETA ** (-jnp.arange(0, R, 2, dtype=jnp.float32) / R)
            ang = jnp.arange(seq_len, dtype=jnp.float32)[:, None] * inv_freq
            cos = jnp.concatenate([jnp.cos(ang), jnp.cos(ang)], axis=-1)
            sin = jnp.concatenate([jnp.sin(ang), jnp.sin(ang)], axis=-1)
            return (cos.astype(dtype), sin.astype(dtype))

        def apply_rope(x, cos, sin):
            x1, x2 = jnp.split(x, 2, axis=-1)
            rot = jnp.concatenate([-x2, x1], axis=-1)
            return x * cos + rot * sin

        def _reference_tuple_inner(x, W_dq, W_uq, W_qr, W_dkv, W_ukv, W_kr, W_o, q_ln_g, q_ln_b, kv_ln_g, kv_ln_b):
            b, s, d = x.shape
            cq = layernorm(x @ W_dq, q_ln_g, q_ln_b)
            Q = (cq @ W_uq).reshape(b, s, N_HEADS, DH).transpose(0, 2, 1, 3)
            Qr = (cq @ W_qr).reshape(b, s, N_HEADS, R).transpose(0, 2, 1, 3)
            cos, sin = rope_cos_sin(s, x.dtype)
            Qr = apply_rope(Qr, cos, sin)
            q = jnp.concatenate([Q, Qr], axis=-1)
            ckv = layernorm(x @ W_dkv, kv_ln_g, kv_ln_b)
            KV = ckv @ W_ukv
            K, V = (KV[..., :D_MODEL], KV[..., D_MODEL:])
            K = K.reshape(b, s, N_HEADS, DH).transpose(0, 2, 1, 3)
            Kr = (x @ W_kr).reshape(b, s, N_HEADS, R).transpose(0, 2, 1, 3)
            Kr = apply_rope(Kr, cos, sin)
            k = jnp.concatenate([K, Kr], axis=-1)
            v = V.reshape(b, s, N_HEADS, DH).transpose(0, 2, 1, 3)
            scale = 1.0 / jnp.sqrt(jnp.asarray(DH + R, x.dtype))
            scores = jnp.einsum('bhqd,bhkd->bhqk', q, k) * scale
            mask = jnp.tril(jnp.ones((s, s), dtype=bool))
            scores = jnp.where(mask, scores, jnp.finfo(scores.dtype).min)
            attn = jax.nn.softmax(scores, axis=-1)
            out = jnp.einsum('bhqk,bhkd->bhqd', attn, v)
            out = out.transpose(0, 2, 1, 3).reshape(b, s, d)
            return (out @ W_o.T, ckv)
        key = jax.random.key(seed)
        ks = jax.random.split(key, 9)
        p = lambda k, shape: 0.01 * jax.random.normal(k, shape, jnp.float32)
        return {'x': jax.random.normal(ks[0], (B, S, D_MODEL), jnp.float32), 'W_dq': p(ks[1], (D_MODEL, Q_PROJ)), 'W_uq': p(ks[2], (Q_PROJ, D_MODEL)), 'W_qr': p(ks[3], (Q_PROJ, ROPE_DIM)), 'W_dkv': p(ks[4], (D_MODEL, KV_PROJ)), 'W_ukv': p(ks[5], (KV_PROJ, 2 * D_MODEL)), 'W_kr': p(ks[6], (D_MODEL, ROPE_DIM)), 'W_o': p(ks[7], (D_MODEL, D_MODEL)), 'q_ln_g': jnp.ones((Q_PROJ,), jnp.float32), 'q_ln_b': jnp.zeros((Q_PROJ,), jnp.float32), 'kv_ln_g': jnp.ones((KV_PROJ,), jnp.float32), 'kv_ln_b': jnp.zeros((KV_PROJ,), jnp.float32)}
    _L0_attn_all = _L0_attn_setup()
    _L0_attn_in = {k: v for k, v in _L0_attn_all.items() if k in ('W_dq', 'W_uq', 'W_qr', 'W_dkv', 'W_ukv', 'W_kr', 'W_o', 'q_ln_g', 'q_ln_b', 'kv_ln_g', 'kv_ln_b')}
    del _L0_attn_all

    def _L0_ffn_setup():
        import jax, jax.numpy as jnp
        import numpy as np
        B, T, D, H = (64, 128, 128, 256)

        def _linear_params(key, out_dim, in_dim):
            kw, kb = jax.random.split(key)
            bound = 1.0 / np.sqrt(in_dim)
            W = jax.random.uniform(kw, (out_dim, in_dim), jnp.float32, -bound, bound)
            b = jax.random.uniform(kb, (out_dim,), jnp.float32, -bound, bound)
            return (W, b)
        key = jax.random.key(seed)
        ks = jax.random.split(key, 8)
        x = jax.random.normal(ks[0], (B, T, D), jnp.float32)
        Wuz, buz = _linear_params(ks[1], H, D)
        Wwz, bwz = _linear_params(ks[2], H, H)
        Wur, bur = _linear_params(ks[3], H, D)
        Wwr, bwr = _linear_params(ks[4], H, H)
        Wu, bu = _linear_params(ks[5], H, D)
        Ww, bw = _linear_params(ks[6], H, H)
        Wo, bo = _linear_params(ks[7], D, H)
        return dict(x=x, Wuz=Wuz, buz=buz, Wwz=Wwz, bwz=bwz, Wur=Wur, bur=bur, Wwr=Wwr, bwr=bwr, Wu=Wu, bu=bu, Ww=Ww, bw=bw, Wo=Wo, bo=bo)
    _L0_ffn_all = _L0_ffn_setup()
    _L0_ffn_in = {k: v for k, v in _L0_ffn_all.items() if k in ('Wuz', 'buz', 'Wwz', 'bwz', 'Wur', 'bur', 'Wwr', 'bwr', 'Wu', 'bu', 'Ww', 'bw', 'Wo', 'bo')}
    del _L0_ffn_all
    return {'x': x, 'L0_tok_W': _L0_tok_in['W'], 'L0_tok_b': _L0_tok_in['b'], 'L0_tok_gamma': _L0_tok_in['gamma'], 'L0_tok_beta': _L0_tok_in['beta'], 'L0_attn_W_dq': _L0_attn_in['W_dq'], 'L0_attn_W_uq': _L0_attn_in['W_uq'], 'L0_attn_W_qr': _L0_attn_in['W_qr'], 'L0_attn_W_dkv': _L0_attn_in['W_dkv'], 'L0_attn_W_ukv': _L0_attn_in['W_ukv'], 'L0_attn_W_kr': _L0_attn_in['W_kr'], 'L0_attn_W_o': _L0_attn_in['W_o'], 'L0_attn_q_ln_g': _L0_attn_in['q_ln_g'], 'L0_attn_q_ln_b': _L0_attn_in['q_ln_b'], 'L0_attn_kv_ln_g': _L0_attn_in['kv_ln_g'], 'L0_attn_kv_ln_b': _L0_attn_in['kv_ln_b'], 'L0_ffn_Wuz': _L0_ffn_in['Wuz'], 'L0_ffn_buz': _L0_ffn_in['buz'], 'L0_ffn_Wwz': _L0_ffn_in['Wwz'], 'L0_ffn_bwz': _L0_ffn_in['bwz'], 'L0_ffn_Wur': _L0_ffn_in['Wur'], 'L0_ffn_bur': _L0_ffn_in['bur'], 'L0_ffn_Wwr': _L0_ffn_in['Wwr'], 'L0_ffn_bwr': _L0_ffn_in['bwr'], 'L0_ffn_Wu': _L0_ffn_in['Wu'], 'L0_ffn_bu': _L0_ffn_in['bu'], 'L0_ffn_Ww': _L0_ffn_in['Ww'], 'L0_ffn_bw': _L0_ffn_in['bw'], 'L0_ffn_Wo': _L0_ffn_in['Wo'], 'L0_ffn_bo': _L0_ffn_in['bo']}

def reference(x, L0_tok_W, L0_tok_b, L0_tok_gamma, L0_tok_beta, L0_attn_W_dq, L0_attn_W_uq, L0_attn_W_qr, L0_attn_W_dkv, L0_attn_W_ukv, L0_attn_W_kr, L0_attn_W_o, L0_attn_q_ln_g, L0_attn_q_ln_b, L0_attn_kv_ln_g, L0_attn_kv_ln_b, L0_ffn_Wuz, L0_ffn_buz, L0_ffn_Wwz, L0_ffn_bwz, L0_ffn_Wur, L0_ffn_bur, L0_ffn_Wwr, L0_ffn_bwr, L0_ffn_Wu, L0_ffn_bu, L0_ffn_Ww, L0_ffn_bw, L0_ffn_Wo, L0_ffn_bo):
    import jax
    import jax.numpy as jnp

    def _L0_tok_ref(x, W, b, gamma, beta):
        import jax, jax.numpy as jnp
        import numpy as np
        PATCH_LENGTH = 128
        PATCH_STRIDE = 64
        MODEL_DIM = 128
        LN_EPS = 0.001
        B, T, C = x.shape
        num_patches = (T - PATCH_LENGTH) // PATCH_STRIDE + 1
        idx = jnp.arange(num_patches)[:, None] * PATCH_STRIDE + jnp.arange(PATCH_LENGTH)[None, :]
        patches = x[:, idx, :]
        patches = patches.reshape(B, num_patches, PATCH_LENGTH * C)
        proj = jnp.einsum('bpf,fd->bpd', patches, W) + b
        mean = jnp.mean(proj, axis=-1, keepdims=True)
        var = jnp.mean(jnp.square(proj - mean), axis=-1, keepdims=True)
        out = (proj - mean) * jax.lax.rsqrt(var + LN_EPS) * gamma + beta
        return out

    def _L0_attn_ref(x, W_dq, W_uq, W_qr, W_dkv, W_ukv, W_kr, W_o, q_ln_g, q_ln_b, kv_ln_g, kv_ln_b):
        import jax, jax.numpy as jnp
        import numpy as np
        D_MODEL = 128
        N_HEADS = 8
        DH = D_MODEL // N_HEADS
        Q_PROJ = D_MODEL // 2
        KV_PROJ = 2 * D_MODEL // 3
        ROPE_DIM = D_MODEL // 8
        R = ROPE_DIM // N_HEADS
        THETA = 10000.0
        EPS = 1e-05
        B, S = (2, 512)

        def layernorm(x, g, b):
            m = jnp.mean(x, axis=-1, keepdims=True)
            v = jnp.var(x, axis=-1, keepdims=True)
            return (x - m) * jax.lax.rsqrt(v + EPS) * g + b

        def rope_cos_sin(seq_len, dtype):
            inv_freq = THETA ** (-jnp.arange(0, R, 2, dtype=jnp.float32) / R)
            ang = jnp.arange(seq_len, dtype=jnp.float32)[:, None] * inv_freq
            cos = jnp.concatenate([jnp.cos(ang), jnp.cos(ang)], axis=-1)
            sin = jnp.concatenate([jnp.sin(ang), jnp.sin(ang)], axis=-1)
            return (cos.astype(dtype), sin.astype(dtype))

        def apply_rope(x, cos, sin):
            x1, x2 = jnp.split(x, 2, axis=-1)
            rot = jnp.concatenate([-x2, x1], axis=-1)
            return x * cos + rot * sin

        def _reference_tuple_inner(x, W_dq, W_uq, W_qr, W_dkv, W_ukv, W_kr, W_o, q_ln_g, q_ln_b, kv_ln_g, kv_ln_b):
            b, s, d = x.shape
            cq = layernorm(x @ W_dq, q_ln_g, q_ln_b)
            Q = (cq @ W_uq).reshape(b, s, N_HEADS, DH).transpose(0, 2, 1, 3)
            Qr = (cq @ W_qr).reshape(b, s, N_HEADS, R).transpose(0, 2, 1, 3)
            cos, sin = rope_cos_sin(s, x.dtype)
            Qr = apply_rope(Qr, cos, sin)
            q = jnp.concatenate([Q, Qr], axis=-1)
            ckv = layernorm(x @ W_dkv, kv_ln_g, kv_ln_b)
            KV = ckv @ W_ukv
            K, V = (KV[..., :D_MODEL], KV[..., D_MODEL:])
            K = K.reshape(b, s, N_HEADS, DH).transpose(0, 2, 1, 3)
            Kr = (x @ W_kr).reshape(b, s, N_HEADS, R).transpose(0, 2, 1, 3)
            Kr = apply_rope(Kr, cos, sin)
            k = jnp.concatenate([K, Kr], axis=-1)
            v = V.reshape(b, s, N_HEADS, DH).transpose(0, 2, 1, 3)
            scale = 1.0 / jnp.sqrt(jnp.asarray(DH + R, x.dtype))
            scores = jnp.einsum('bhqd,bhkd->bhqk', q, k) * scale
            mask = jnp.tril(jnp.ones((s, s), dtype=bool))
            scores = jnp.where(mask, scores, jnp.finfo(scores.dtype).min)
            attn = jax.nn.softmax(scores, axis=-1)
            out = jnp.einsum('bhqk,bhkd->bhqd', attn, v)
            out = out.transpose(0, 2, 1, 3).reshape(b, s, d)
            return (out @ W_o.T, ckv)
        return _reference_tuple_inner(x, W_dq, W_uq, W_qr, W_dkv, W_ukv, W_kr, W_o, q_ln_g, q_ln_b, kv_ln_g, kv_ln_b)[0]

    def _L0_ffn_ref(x, Wuz, buz, Wwz, bwz, Wur, bur, Wwr, bwr, Wu, bu, Ww, bw, Wo, bo):
        import jax, jax.numpy as jnp
        import numpy as np
        B, T, D, H = (64, 128, 128, 256)

        def _linear_params(key, out_dim, in_dim):
            kw, kb = jax.random.split(key)
            bound = 1.0 / np.sqrt(in_dim)
            W = jax.random.uniform(kw, (out_dim, in_dim), jnp.float32, -bound, bound)
            b = jax.random.uniform(kb, (out_dim,), jnp.float32, -bound, bound)
            return (W, b)
        b_, t_, _ = x.shape
        h_dim = Wwz.shape[0]
        xz = (jnp.einsum('btd,hd->bth', x, Wuz) + buz).transpose(1, 0, 2)
        xr = (jnp.einsum('btd,hd->bth', x, Wur) + bur).transpose(1, 0, 2)
        xc = (jnp.einsum('btd,hd->bth', x, Wu) + bu).transpose(1, 0, 2)

        def step(h, inp):
            xz_t, xr_t, xc_t = inp
            z = jax.nn.sigmoid(xz_t + h @ Wwz.T + bwz)
            r = jax.nn.sigmoid(xr_t + h @ Wwr.T + bwr)
            c = jnp.tanh(xc_t + h * r @ Ww.T + bw)
            h_new = z * h + (1.0 - z) * c
            return (h_new, h_new)
        h0 = jnp.zeros((b_, h_dim), x.dtype)
        _, hs = jax.lax.scan(step, h0, (xz, xr, xc))
        out = jax.nn.sigmoid(jnp.einsum('tbh,dh->btd', hs, Wo) + bo)
        return out
    h = _L0_tok_ref(x, L0_tok_W, L0_tok_b, L0_tok_gamma, L0_tok_beta)
    h = h + _L0_attn_ref(_layernorm(h, axis=-1), L0_attn_W_dq, L0_attn_W_uq, L0_attn_W_qr, L0_attn_W_dkv, L0_attn_W_ukv, L0_attn_W_kr, L0_attn_W_o, L0_attn_q_ln_g, L0_attn_q_ln_b, L0_attn_kv_ln_g, L0_attn_kv_ln_b)
    h = h + _L0_ffn_ref(_layernorm(h, axis=-1), L0_ffn_Wuz, L0_ffn_buz, L0_ffn_Wwz, L0_ffn_bwz, L0_ffn_Wur, L0_ffn_bur, L0_ffn_Wwr, L0_ffn_bwr, L0_ffn_Wu, L0_ffn_bu, L0_ffn_Ww, L0_ffn_bw, L0_ffn_Wo, L0_ffn_bo)
    return h

_drawn_inputs = setup_inputs


def setup_inputs(seed=0):
    import zlib

    import numpy as np

    out = dict(_drawn_inputs(seed))
    spreads = {'L0_tok_b': (0.0, 0.1),
     'L0_tok_gamma': (1.0, 0.2),
     'L0_tok_beta': (0.0, 0.1),
     'L0_attn_q_ln_g': (1.0, 0.6),
     'L0_attn_q_ln_b': (0.0, 0.8),
     'L0_attn_kv_ln_g': (1.0, 0.6),
     'L0_attn_kv_ln_b': (0.0, 0.8)}
    factors = {'L0_attn_W_dq': 8.0,
     'L0_attn_W_uq': 8.0,
     'L0_attn_W_qr': 8.0,
     'L0_attn_W_dkv': 8.0,
     'L0_attn_W_ukv': 8.0,
     'L0_attn_W_kr': 8.0,
     'L0_attn_W_o': 8.0,
     'L0_ffn_Wuz': 5.615,
     'L0_ffn_buz': 23.181,
     'L0_ffn_Wwz': 8.0,
     'L0_ffn_bwz': 27.154,
     'L0_ffn_Wur': 8.0,
     'L0_ffn_bur': 28.752,
     'L0_ffn_Wwr': 8.0,
     'L0_ffn_bwr': 37.757,
     'L0_ffn_bu': 8.0,
     'L0_ffn_Ww': 8.0,
     'L0_ffn_bw': 8.0,
     'L0_ffn_bo': 7.016}
    for name, (base, spread) in spreads.items():
        noise = np.random.default_rng([zlib.crc32(name.encode()), seed]).standard_normal(out[name].shape)
        drawn = base * np.exp(spread * noise) if base else spread * noise
        out[name] = jnp.asarray(drawn.astype(out[name].dtype))
    for name, factor in factors.items():
        out[name] = (out[name] * factor).astype(out[name].dtype)
    return out
```

```python
from contextlib import ExitStack

import numpy as np

import concourse.bass as bass
from concourse import mybir

F32 = mybir.dt.float32
ALU = mybir.AluOpType
ACT = mybir.ActivationFunctionType
AX_X = mybir.AxisListType.X

B = 64
T = 10
NT = T // 2
D = 128
PATCH = 256
HEADS, DH, R = 8, 16, 2
HD = DH + R
DQ, DKV = D // 2, 2 * D // 3
H = 256
KC = H // 128
SCALE = float(HD) ** -0.5
LOWEST = float(np.finfo(np.float32).min)
EPS_TOK, EPS = 1e-3, 1e-5

TOKW = 0
WDOWN = TOKW + 2 * D
WKR = WDOWN + DQ + DKV
WOUT = WKR + HEADS * R
PACK_A = WOUT + D
WX = 0
WH = WX + 3 * H
WO = WH + 3 * KC * H
BIAS_X = WO + KC * D
BIAS_H = BIAS_X + 3 * KC
PACK_G = BIAS_H + 3 * KC

ORDER = [("x_turn", 0), ("x_turn", 1)]
for j in range(NT):
    ORDER += [(s, j) for s in ("proj", "norm_tok", "norm_pre", "x_norm_turn", "down", "norm_down", "down_turn",
                               "up", "rope")]
for j in range(NT):
    ORDER += [(s, j) for s in ("scores", "softmax", "mix", "mix_turn", "attn_out", "norm_gru", "gru_in_turn")]
    for t in (2 * j, 2 * j + 1):
        ORDER += [("gru", t)]
    ORDER += [("out", j)]


def audio_tower(nc, x, pack_a, pack_q, pack_kv, rows, pack_g, rope_q, rope_k, out):
    with ExitStack() as ctx:
        def sb(name, shape):
            return ctx.enter_context(nc.sbuf_tensor(name, shape, F32))

        def bank(name):
            return ctx.enter_context(nc.psum_tensor(name, [128, 512], F32))

        def sem(name):
            return ctx.enter_context(nc.semaphore(name))

        w_a = sb("w_a", [128, PACK_A])
        w_q = sb("w_q", [DQ, HEADS * HD + 2])
        w_kv = sb("w_kv", [DKV, 2 * D + 2])
        w_g = sb("w_g", [128, PACK_G])
        w_hs = sb("w_hs", [128, 3 * KC * H + KC * D])
        half_bias = sb("half_bias", [128, 3 * KC])
        row_b = sb("row_b", [1, 2 * D])
        gamma_b = sb("gamma_b", [128, 2 * D])
        rq = sb("rq", [128, NT, 2, HEADS * R])
        rk = sb("rk", [128, NT, 2, 2, HEADS * R])
        ident = sb("ident", [128, 128])
        ones = sb("ones", [1, 128])
        minus_half = sb("minus_half", [128, 2])
        x_sb = sb("x_sb", [128, NT + 1, D])
        xT = sb("xT", [128, (T + 1) * B])
        hn = sb("hn", [128, NT, D])
        hg = sb("hg", [128, NT, D])
        h1 = sb("h1", [128, NT, D])
        xn = sb("xn", [128, NT, D])
        xnT = sb("xnT", [128, NT, D])
        cn = sb("cn", [128, NT, DQ + DKV])
        cqT = sb("cqT", [DQ, NT, D])
        ckvT = sb("ckvT", [DKV, NT, 2, 2 * B])
        xnT2 = sb("xnT2", [128, NT, 2, 2 * B])
        q = sb("q", [128, NT, HEADS, HD])
        k = sb("k", [128, T, HEADS, HD])
        v = sb("v", [128, T, HEADS, DH])
        swap_q = sb("swap_q", [128, NT, HEADS, R])
        swap_k = sb("swap_k", [128, NT, 2, HEADS * R])
        cos_k = sb("cos_k", [128, NT, 2, HEADS * R])
        prod = sb("prod", [128, T, HEADS, HD])
        sc = sb("sc", [128, T, HEADS])
        scm = sb("scm", [128, T, HEADS])
        p = sb("p", [128, T, HEADS])
        mx = sb("mx", [128, HEADS])
        den = sb("den", [128, HEADS])
        rden = sb("rden", [128, HEADS])
        prod_v = sb("prod_v", [128, T, HEADS, DH])
        mixed = sb("mixed", [128, D])
        on = sb("on", [128, NT, D])
        onT = sb("onT", [128, NT, D])
        h2 = sb("h2", [128, NT, D])
        h2h = sb("h2h", [128, NT, D])
        xg = sb("xg", [128, NT, D])
        xgT = sb("xgT", [128, T, B])
        stats = sb("stats", [128, NT, 5, 6])
        mv = sb("mv", [128, NT, 5, 2])
        ve = sb("ve", [128, NT, 5])
        rstd = sb("rstd", [128, NT, 5])
        hs = sb("hs", [128, KC, T, B])
        tr = sb("tr", [128, KC, B])
        tz = sb("tz", [128, KC, B])
        tc = sb("tc", [128, KC, B])
        rh = sb("rh", [128, KC, B])
        keep = sb("keep", [128, KC, B])
        move = sb("move", [128, KC, B])
        ot = sb("ot", [128, NT, D])
        o = sb("o", [128, NT, D])

        turn_ps = bank("turn_ps")
        mm_ps = bank("mm_ps")
        down_ps = bank("down_ps")
        kv_ps = bank("kv_ps")
        rz_ps = [bank(f"rz_ps{m}") for m in range(KC)]
        c_ps = [bank(f"c_ps{m}") for m in range(KC)]
        Q0 = 160
        KR0 = Q0 + HEADS * HD
        CQ0 = KR0 + 2 * HEADS * R

        s_x = [sem(f"s_x{i}") for i in range(2)]
        s_wa = sem("s_wa")
        s_wq = sem("s_wq")
        s_wkv = sem("s_wkv")
        s_rows = sem("s_rows")
        s_gamma = sem("s_gamma")
        s_rope = sem("s_rope")
        s_wg = sem("s_wg")
        s_const = sem("s_const")
        s_ident = sem("s_ident")
        s_scaled = sem("s_scaled")
        s_hbias = sem("s_hbias")
        s_xT_ps = sem("s_xT_ps")
        s_xT = sem("s_xT")
        s_proj = sem("s_proj")
        NORMS = ("tok", "pre", "q", "kv", "gru")
        s_stats = {n: sem(f"s_stats_{n}") for n in NORMS}
        s_mv = {n: sem(f"s_mv_{n}") for n in NORMS}
        s_ve = {n: sem(f"s_ve_{n}") for n in NORMS}
        s_rstd = {n: sem(f"s_rstd_{n}") for n in NORMS}
        s_hn = sem("s_hn")
        s_hg = sem("s_hg")
        s_h1 = sem("s_h1")
        s_xn = sem("s_xn")
        s_xnT_ps = sem("s_xnT_ps")
        s_xnT = sem("s_xnT")
        s_xnT2 = sem("s_xnT2")
        s_down = sem("s_down")
        s_cn = sem("s_cn")
        s_cqT_ps = sem("s_cqT_ps")
        s_ckvT_ps = sem("s_ckvT_ps")
        s_cqT = sem("s_cqT")
        s_ckvT = sem("s_ckvT")
        s_up_q = sem("s_up_q")
        s_up_kv = sem("s_up_kv")
        s_q_plain = sem("s_q_plain")
        s_swap = sem("s_swap")
        s_q_rot = sem("s_q_rot")
        s_k_rot = sem("s_k_rot")
        s_k = sem("s_k")
        s_v = sem("s_v")
        s_prod = sem("s_prod")
        s_sc = sem("s_sc")
        s_masked = sem("s_masked")
        s_mx = sem("s_mx")
        s_scm = sem("s_scm")
        s_p = sem("s_p")
        s_den = sem("s_den")
        s_rden = sem("s_rden")
        s_prod_v = sem("s_prod_v")
        s_mixed = sem("s_mixed")
        s_on = sem("s_on")
        s_onT_ps = sem("s_onT_ps")
        s_onT = sem("s_onT")
        s_attn = sem("s_attn")
        s_h2 = sem("s_h2")
        s_h2h = sem("s_h2h")
        s_xg = sem("s_xg")
        s_xgT_ps = sem("s_xgT_ps")
        s_xgT = sem("s_xgT")
        s_r_ps = [sem(f"s_r_ps{m}") for m in range(KC)]
        s_z_ps = [sem(f"s_z_ps{m}") for m in range(KC)]
        s_c_ps = [sem(f"s_c_ps{m}") for m in range(KC)]
        s_tr = [sem(f"s_tr{m}") for m in range(KC)]
        s_tz = [sem(f"s_tz{m}") for m in range(KC)]
        s_tc = [sem(f"s_tc{m}") for m in range(KC)]
        s_rh = [sem(f"s_rh{m}") for m in range(KC)]
        s_keep = sem("s_keep")
        s_move = [sem(f"s_move{m}") for m in range(KC)]
        s_hs = [sem(f"s_hs{m}") for m in range(KC)]
        s_out_ps = sem("s_out_ps")
        s_ot = sem("s_ot")
        s_o = sem("s_o")
        s_stored = sem("s_stored")

        block = ctx.enter_context(nc.Block())

        def w_x(g, m):
            return w_g[:, WX + g * H + m * 128:WX + g * H + (m + 1) * 128]

        def w_h(g, kc, m):
            at = (g * KC + kc) * H + m * 128
            return w_hs[:, at:at + 128]

        def w_o(kc):
            at = 3 * KC * H + kc * D
            return w_hs[:, at:at + D]

        RG, ZG, CG = range(3)

        @block.sync
        def _(sp):
            even = x[:, 0:T * D].rearrange("b (j c) -> b j c", c=2 * D)
            sp.dma_start(x_sb[0:B, 0:NT, :], even[:, :, 0:D]).then_inc(s_x[0], 16)
            sp.dma_start(x_sb[B:128, 0:NT, :], even[:, :, D:2 * D]).then_inc(s_x[0], 16)
            sp.dma_start(x_sb[0:B, NT, :], x[:, T * D:(T + 1) * D]).then_inc(s_x[1], 16)
            sp.dma_start(gamma_b[:, :], rows[1:2, :].broadcast_to([128, 2 * D])).then_inc(s_gamma, 16)
            sp.dma_start(rq[:, :, :, :], rope_q).then_inc(s_rope, 16)
            sp.dma_start(rk[:, :, :, :, :], rope_k).then_inc(s_rope, 16)
            sp.dma_start(w_g[:, :], pack_g).then_inc(s_wg, 16)
            for stage, j in ORDER:
                if stage == "out":
                    sp.wait_ge(s_o, j + 1)
                    for par in range(2):
                        sp.dma_start(out[:, 2 * j + par, :], o[par * B:(par + 1) * B, j, :]).then_inc(s_stored, 16)
            sp.wait_ge(s_stored, 16 * T)

        @block.gpsimd
        def _(pool):
            nc.gpsimd.memset(ident[:, :], 0.0).then_inc(s_const, 1)
            nc.gpsimd.memset(ones[:, :], 1.0).then_inc(s_const, 1)
            nc.gpsimd.memset(minus_half[:, :], -0.5).then_inc(s_const, 1)
            pool.wait_ge(s_const, 3)
            nc.gpsimd.affine_select(out=ident[:, :], in_=ident[:, :], compare_op=ALU.not_equal, fill=1.0, base=0,
                                    pattern=[[-1, 128]], channel_multiplier=1).then_inc(s_ident, 1)

            def power(j, norms, at, n):
                for name in norms:
                    pool.wait_ge(s_ve[name], j + 1)
                ins = nc.gpsimd.tensor_tensor(rstd[:, j, at:at + n], ve[:, j, at:at + n], minus_half[:, 0:n],
                                              ALU.pow)
                ins.then_inc(s_rstd[norms[0]], 1)

            for stage, j in ORDER:
                if stage == "norm_tok":
                    power(j, ("tok",), 0, 1)
                if stage == "norm_pre":
                    power(j, ("pre",), 1, 1)
                if stage == "down":
                    pool.wait_ge(s_xnT, j + 1)
                    nc.gpsimd.tensor_copy(xnT2[:, j, :, :].rearrange("p s (e b) -> p s e b", e=2),
                                          xnT[:, j, :].rearrange("p (s b) -> p s b", s=2).unsqueeze(2)
                                          .broadcast_to([128, 2, 2, B])).then_inc(s_xnT2, 1)
                if stage == "norm_down":
                    power(j, ("q", "kv"), 2, 2)
                    if j == 0:
                        pool.wait_ge(s_wg, 16)
                        nc.gpsimd.tensor_scalar(w_hs[:, 0:2 * KC * H], w_g[:, WH:WH + 2 * KC * H], 0.5, None,
                                                ALU.mult).then_inc(s_scaled, 1)
                        nc.gpsimd.tensor_scalar(w_hs[:, 2 * KC * H:3 * KC * H],
                                                w_g[:, WH + 2 * KC * H:WH + 3 * KC * H], 0.25, None,
                                                ALU.mult).then_inc(s_scaled, 1)
                        nc.gpsimd.tensor_scalar(w_hs[:, 3 * KC * H:], w_g[:, WO:WO + KC * D], 0.5, None,
                                                ALU.mult).then_inc(s_scaled, 1)
                if stage == "norm_gru":
                    power(j, ("gru",), 4, 1)
                    pool.wait_ge(s_h2, j + 1)
                    nc.gpsimd.tensor_scalar(h2h[:, j, :], h2[:, j, :], 0.5, None, ALU.add).then_inc(s_h2h, 1)

        @block.scalar
        def _(act):
            act.dma_start(w_a[:, :], pack_a).then_inc(s_wa, 16)
            act.dma_start(row_b[:, :], rows[0:1, :]).then_inc(s_rows, 16)
            act.dma_start(w_q[:, :], pack_q).then_inc(s_wq, 16)
            act.dma_start(w_kv[:, :], pack_kv).then_inc(s_wkv, 16)
            for stage, j in ORDER:
                if stage == "x_turn":
                    cols = slice(0, 512) if j == 0 else slice(512, (T + 1) * B)
                    act.wait_ge(s_xT_ps, j + 1)
                    src = turn_ps[:, 0:512] if j == 0 else mm_ps[:, 0:(T + 1) * B - 512]
                    nc.scalar.copy(xT[:, cols], src).then_inc(s_xT, 1)
                if stage == "x_norm_turn":
                    act.wait_ge(s_xnT_ps, j + 1)
                    nc.scalar.copy(xnT[:, j, :], turn_ps[:, 0:D]).then_inc(s_xnT, 1)
                if stage == "down_turn":
                    act.wait_ge(s_ckvT_ps, j + 1)
                    if j == 0:
                        act.wait_ge(s_wkv, 16)
                    nc.scalar.activation(ckvT[:, j, :, :].rearrange("p s (e b) -> p s e b", e=2),
                                         turn_ps[0:DKV, 0:D].rearrange("p (s b) -> p s b", s=2).unsqueeze(2)
                                         .broadcast_to([DKV, 2, 2, B]), ACT.Identity,
                                         bias=w_kv[:, 2 * D + 1:2 * D + 2], scale=w_kv[:, 2 * D:2 * D + 1]) \
                        .then_inc(s_ckvT, 1)
                if stage == "up":
                    act.wait_ge(s_up_kv, j + 1)
                    kv = kv_ps[:, :].rearrange("p (s e h d) -> p s e h d", s=2, e=2, h=HEADS)
                    nc.scalar.copy(k[:, 2 * j:2 * j + 2, :, 0:DH], kv[:, :, 0, :, :]).then_inc(s_k, 1)
                    nc.scalar.copy(v[:, 2 * j:2 * j + 2, :, :], kv[:, :, 1, :, :]).then_inc(s_v, 1)
                if stage == "softmax":
                    act.wait_ge(s_scm, j + 1)
                    S = 2 * j + 2
                    nc.scalar.activation(p[:, 0:S, :], scm[:, 0:S, :], ACT.Exp, scale=SCALE).then_inc(s_p, 1)
                if stage == "mix_turn":
                    act.wait_ge(s_onT_ps, j + 1)
                    nc.scalar.copy(onT[:, j, :], turn_ps[:, 0:D]).then_inc(s_onT, 1)
                if stage == "gru_in_turn":
                    act.wait_ge(s_xgT_ps, j + 1)
                    nc.scalar.copy(xgT[:, 2 * j:2 * j + 2, :],
                                   turn_ps[:, 0:D].rearrange("p (s b) -> p s b", s=2)).then_inc(s_xgT, 1)
                if stage == "gru":
                    t = j
                    if t == 0:
                        act.wait_ge(s_hbias, 2)
                    for m in range(KC) if t else ():
                        act.wait_ge(s_r_ps[m], t)
                        nc.scalar.activation(tr[:, m, :], rz_ps[m][:, 0:B], ACT.Tanh, scale=0.5,
                                             bias=half_bias[:, m:m + 1]).then_inc(s_tr[m], 1)
                    for m in range(KC):
                        act.wait_ge(s_z_ps[m], t + 1)
                        nc.scalar.activation(tz[:, m, :], rz_ps[m][:, B:2 * B], ACT.Tanh, scale=0.5,
                                             bias=half_bias[:, KC + m:KC + m + 1]).then_inc(s_tz[m], 1)
                    for m in range(KC):
                        act.wait_ge(s_c_ps[m], t + 1)
                        nc.scalar.activation(tc[:, m, :], c_ps[m][:, 0:B], ACT.Tanh,
                                             bias=half_bias[:, 2 * KC + m:2 * KC + m + 1]).then_inc(s_tc[m], 1)
                if stage == "out":
                    act.wait_ge(s_out_ps, j + 1)
                    nc.scalar.activation(ot[:, j, :], mm_ps[:, 0:D], ACT.Tanh, scale=0.5).then_inc(s_ot, 1)

        @block.vector
        def _(dve):
            def moments(j, name, at, src):
                nc.vector.bn_stats(stats[:, j, at, :], src).then_inc(s_stats[name], 1)
                dve.wait_ge(s_stats[name], j + 1)
                nc.vector.bn_aggr(mv[:, j, at, :], stats[:, j, at, :]).then_inc(s_mv[name], 1)
                dve.wait_ge(s_mv[name], j + 1)
                nc.vector.tensor_scalar(ve[:, j, at:at + 1], mv[:, j, at, 1:2], EPS_TOK if name == "tok" else EPS,
                                        None, ALU.add).then_inc(s_ve[name], 1)

            def normed(dst, src, j, at):
                return nc.vector.tensor_scalar(dst, src, mv[:, j, at, 0:1], rstd[:, j, at:at + 1], ALU.subtract,
                                               ALU.mult)

            for stage, j in ORDER:
                if stage == "norm_tok":
                    dve.wait_ge(s_proj, j + 1)
                    moments(j, "tok", 0, mm_ps[:, 0:D])
                    dve.wait_ge(s_rstd["tok"], j + 1)
                    normed(hn[:, j, :], mm_ps[:, 0:D], j, 0).then_inc(s_hn, 1)
                    dve.wait_ge(s_hn, j + 1)
                    if j == 0:
                        dve.wait_ge(s_gamma, 16)
                    nc.vector.tensor_tensor(hg[:, j, :], hn[:, j, :], gamma_b[:, 0:D], ALU.mult).then_inc(s_hg, 1)
                    dve.wait_ge(s_hg, j + 1)
                    nc.vector.tensor_tensor(h1[:, j, :], hg[:, j, :], gamma_b[:, D:2 * D], ALU.add) \
                        .then_inc(s_h1, 1)
                if stage == "norm_pre":
                    dve.wait_ge(s_h1, j + 1)
                    moments(j, "pre", 1, h1[:, j, :])
                    dve.wait_ge(s_rstd["pre"], j + 1)
                    normed(xn[:, j, :], h1[:, j, :], j, 1).then_inc(s_xn, 1)
                if stage == "norm_down":
                    dve.wait_ge(s_down, j + 1)
                    moments(j, "q", 2, down_ps[:, 0:DQ])
                    moments(j, "kv", 3, down_ps[:, DQ:DQ + DKV])
                    dve.wait_ge(s_rstd["q"], j + 1)
                    normed(cn[:, j, 0:DQ], down_ps[:, 0:DQ], j, 2)
                    normed(cn[:, j, DQ:], down_ps[:, DQ:DQ + DKV], j, 3).then_inc(s_cn, 1)
                if stage == "down_turn":
                    dve.wait_ge(s_cqT_ps, j + 1)
                    if j == 0:
                        dve.wait_ge(s_wq, 16)
                    nc.vector.tensor_scalar(cqT[:, j, :], down_ps[0:DQ, CQ0:CQ0 + D], w_q[:, HEADS * HD:HEADS * HD + 1],
                                            w_q[:, HEADS * HD + 1:HEADS * HD + 2], ALU.mult, ALU.add) \
                        .then_inc(s_cqT, 1)
                if stage == "rope":
                    dve.wait_ge(s_up_q, j + 1)
                    if j == 0:
                        dve.wait_ge(s_rope, 32)
                    qp = down_ps[:, Q0:Q0 + HEADS * HD].rearrange("p (h d) -> p h d", h=HEADS)
                    kp = down_ps[:, KR0:KR0 + 2 * HEADS * R].rearrange("p (s h r) -> p s h r", s=2, r=R)
                    nc.vector.tensor_copy(q[:, j, :, 0:DH], qp[:, :, 0:DH]).then_inc(s_q_plain, 1)
                    sin_q = rq[:, j, 1, :].rearrange("p (h r) -> p h r", r=R)
                    for r in range(R):
                        nc.vector.tensor_tensor(swap_q[:, j, :, r], qp[:, :, DH + 1 - r], sin_q[:, :, r], ALU.mult) \
                            .then_inc(s_swap, 1)
                    sin_k = rk[:, j, 1, :, :].rearrange("p s (h r) -> p s h r", r=R)
                    sk = swap_k[:, j, :, :].rearrange("p s (h r) -> p s h r", r=R)
                    for r in range(R):
                        nc.vector.tensor_tensor(sk[:, :, :, r], kp[:, :, :, 1 - r], sin_k[:, :, :, r], ALU.mult) \
                            .then_inc(s_swap, 1)
                    nc.vector.tensor_tensor(cos_k[:, j, :, :],
                                            down_ps[:, KR0:KR0 + 2 * HEADS * R].rearrange("p (s c) -> p s c", s=2),
                                            rk[:, j, 0, :, :], ALU.mult).then_inc(s_swap, 1)
                    dve.wait_ge(s_swap, 5 * (j + 1))
                    nc.vector.scalar_tensor_tensor(out=q[:, j, :, DH:HD], in0=qp[:, :, DH:HD],
                                                   scalar=rq[:, j, 0, 0:1], in1=swap_q[:, j, :, :],
                                                   op0=ALU.mult, op1=ALU.add).then_inc(s_q_rot, 1)
                    nc.vector.tensor_tensor(k[:, 2 * j:2 * j + 2, :, DH:HD],
                                            cos_k[:, j, :, :].rearrange("p s (h r) -> p s h r", r=R), sk,
                                            ALU.add).then_inc(s_k_rot, 1)
                S = 2 * j + 2
                if stage == "scores":
                    dve.wait_ge(s_q_rot, j + 1)
                    dve.wait_ge(s_q_plain, j + 1)
                    dve.wait_ge(s_k_rot, j + 1)
                    dve.wait_ge(s_k, j + 1)
                    flat = "p s h d -> p s (h d)"
                    qj = q[:, j:j + 1, :, :].rearrange(flat).broadcast_to([128, S, HEADS * HD])
                    nc.vector.tensor_tensor(prod[:, 0:S, :, :].rearrange(flat), k[:, 0:S, :, :].rearrange(flat), qj,
                                            ALU.mult).then_inc(s_prod, 1)
                    dve.wait_ge(s_prod, j + 1)
                    nc.vector.tensor_reduce(sc[:, 0:S, :], prod[:, 0:S, :, :], AX_X, ALU.add).then_inc(s_sc, 1)
                    dve.wait_ge(s_sc, j + 1)
                    nc.vector.memset(sc[0:B, S - 1, :], LOWEST).then_inc(s_masked, 1)
                if stage == "softmax":
                    dve.wait_ge(s_masked, j + 1)
                    nc.vector.tensor_reduce(mx[:, :], sc[:, 0:S, :].rearrange("p s h -> p h s"), AX_X, ALU.max) \
                        .then_inc(s_mx, 1)
                    dve.wait_ge(s_mx, j + 1)
                    if j:
                        dve.wait_ge(s_p, j)
                    nc.vector.tensor_tensor(scm[:, 0:S, :], sc[:, 0:S, :],
                                            mx[:, :].unsqueeze(1).broadcast_to([128, S, HEADS]), ALU.subtract) \
                        .then_inc(s_scm, 1)
                if stage == "mix":
                    dve.wait_ge(s_p, j + 1)
                    dve.wait_ge(s_v, j + 1)
                    vs = v[:, 0:S, :, :].rearrange("p s h d -> p (s h) d")
                    ps = p[:, 0:S, :].rearrange("p s h -> p (s h)").unsqueeze(2)
                    nc.vector.tensor_tensor(prod_v[:, 0:S, :, :].rearrange("p s h d -> p (s h) d"), vs,
                                            ps.broadcast_to([128, S * HEADS, DH]), ALU.mult).then_inc(s_prod_v, 1)
                    nc.vector.tensor_reduce(den[:, :], p[:, 0:S, :].rearrange("p s h -> p h s"), AX_X, ALU.add) \
                        .then_inc(s_den, 1)
                    dve.wait_ge(s_den, j + 1)
                    nc.vector.reciprocal(rden[:, :], den[:, :]).then_inc(s_rden, 1)
                    dve.wait_ge(s_prod_v, j + 1)
                    nc.vector.tensor_reduce(mixed[:, :], prod_v[:, 0:S, :, :].rearrange("p s h d -> p (h d) s"), AX_X,
                                            ALU.add).then_inc(s_mixed, 1)
                    dve.wait_ge(s_mixed, j + 1)
                    dve.wait_ge(s_rden, j + 1)
                    nc.vector.tensor_tensor(on[:, j, :].rearrange("p (h d) -> p h d", h=HEADS),
                                            mixed[:, :].rearrange("p (h d) -> p h d", h=HEADS),
                                            rden[:, :].unsqueeze(2).broadcast_to([128, HEADS, DH]), ALU.mult) \
                        .then_inc(s_on, 1)
                if stage == "norm_gru":
                    dve.wait_ge(s_attn, j + 1)
                    nc.vector.tensor_tensor(h2[:, j, :], mm_ps[:, 0:D], h1[:, j, :], ALU.add).then_inc(s_h2, 1)
                    dve.wait_ge(s_h2, j + 1)
                    moments(j, "gru", 4, h2[:, j, :])
                    dve.wait_ge(s_rstd["gru"], j + 1)
                    normed(xg[:, j, :], h2[:, j, :], j, 4).then_inc(s_xg, 1)
                if stage == "gru":
                    t = j
                    if t == 0:
                        dve.wait_ge(s_wg, 16)
                        bias_sum = half_bias[:, :]
                        nc.vector.tensor_tensor(bias_sum, w_g[:, BIAS_X:BIAS_X + 3 * KC],
                                                w_g[:, BIAS_H:BIAS_H + 3 * KC], ALU.add).then_inc(s_hbias, 1)
                        dve.wait_ge(s_hbias, 1)
                        nc.vector.tensor_scalar(half_bias[:, 0:2 * KC], half_bias[:, 0:2 * KC], 0.5, None,
                                                ALU.mult).then_inc(s_hbias, 1)
                    else:
                        for m in range(KC):
                            dve.wait_ge(s_tr[m], t)
                            dve.wait_ge(s_hs[m], t)
                            nc.vector.scalar_tensor_tensor(out=rh[:, m, :], in0=tr[:, m, :], scalar=1.0,
                                                           in1=hs[:, m, t - 1, :], op0=ALU.add, op1=ALU.mult) \
                                .then_inc(s_rh[m], 1)
                        for m in range(KC):
                            dve.wait_ge(s_tz[m], t + 1)
                        nc.vector.scalar_tensor_tensor(out=keep[:, :, :], in0=tz[:, :, :], scalar=1.0,
                                                       in1=hs[:, :, t - 1, :], op0=ALU.add, op1=ALU.mult) \
                            .then_inc(s_keep, 1)
                    for m in range(KC):
                        dve.wait_ge(s_tc[m], t + 1)
                        dve.wait_ge(s_tz[m], t + 1)
                        nc.vector.scalar_tensor_tensor(out=move[:, m, :], in0=tz[:, m, :], scalar=1.0,
                                                       in1=tc[:, m, :], op0=ALU.subtract, op1=ALU.mult) \
                            .then_inc(s_move[m], 1)
                        dve.wait_ge(s_move[m], t + 1)
                        if t:
                            dve.wait_ge(s_keep, t)
                            nc.vector.scalar_tensor_tensor(out=hs[:, m, t, :], in0=keep[:, m, :], scalar=0.5,
                                                           in1=move[:, m, :], op0=ALU.mult, op1=ALU.subtract) \
                                .then_inc(s_hs[m], 1)
                        else:
                            nc.vector.tensor_scalar(hs[:, m, t, :], move[:, m, :], -1.0, None, ALU.mult) \
                                .then_inc(s_hs[m], 1)
                if stage == "out":
                    dve.wait_ge(s_ot, j + 1)
                    dve.wait_ge(s_h2h, j + 1)
                    nc.vector.scalar_tensor_tensor(out=o[:, j, :], in0=ot[:, j, :], scalar=0.5, in1=h2h[:, j, :],
                                                   op0=ALU.mult, op1=ALU.add).then_inc(s_o, 1)

        @block.tensor
        def _(pe):
            turn_read, mm_read, down_read = [], [], []

            def wait_for(read):
                for s, n in read:
                    pe.wait_ge(s, n)

            def gru_inputs(t):
                pe.wait_ge(s_xgT, t // 2 + 1)
                for m in range(KC):
                    if t:
                        pe.wait_ge(s_tz[m], t)
                    if t > 0:
                        nc.tensor.matmul(rz_ps[m][:, 0:B], w_x(RG, m), xgT[:, t, :], start=True, stop=False,
                                         skip_group_check=True)
                    mm = nc.tensor.matmul(rz_ps[m][:, B:2 * B], w_x(ZG, m), xgT[:, t, :], start=(t == 0),
                                          stop=(t == 0), skip_group_check=True)
                    if t == 0:
                        mm.then_inc(s_z_ps[m], 1)

            pe.wait_ge(s_ident, 1)
            for stage, j in ORDER:
                if stage == "x_turn":
                    pe.wait_ge(s_x[0], 32)
                    if j == 0:
                        for i in range(4):
                            mm = nc.tensor.transpose(turn_ps[:, i * 128:(i + 1) * 128], x_sb[:, i, :], ident[:, :])
                        turn_read = [(s_xT, 1)]
                    else:
                        pe.wait_ge(s_x[1], 16)
                        nc.tensor.transpose(mm_ps[:, 0:128], x_sb[:, 4, :], ident[:, :])
                        mm = nc.tensor.transpose(mm_ps[:, 128:128 + B], x_sb[0:B, 5, :], ident[0:B, 0:B])
                        mm_read = [(s_xT, 2)]
                    mm.then_inc(s_xT_ps, 1)
                if stage == "proj":
                    wait_for(mm_read)
                    if j == 0:
                        pe.wait_ge(s_wa, 16)
                        pe.wait_ge(s_rows, 16)
                        pe.wait_ge(s_const, 3)
                        pe.wait_ge(s_xT, 2)
                    nc.tensor.matmul(mm_ps[:, 0:D], ones[:, :], row_b[:, 0:D], start=True, stop=False)
                    for i in range(2):
                        mm = nc.tensor.matmul(mm_ps[:, 0:D], xT[:, 2 * j * B + i * B:2 * j * B + i * B + 2 * B],
                                              w_a[:, TOKW + i * D:TOKW + (i + 1) * D], start=False, stop=(i == 1))
                    mm.then_inc(s_proj, 1)
                    mm_read = [(s_hn, j + 1)]
                if stage == "x_norm_turn":
                    wait_for(turn_read)
                    pe.wait_ge(s_xn, j + 1)
                    nc.tensor.transpose(turn_ps[:, 0:D], xn[:, j, :], ident[:, :]).then_inc(s_xnT_ps, 1)
                    turn_read = [(s_xnT, j + 1)]
                if stage == "down":
                    wait_for(down_read)
                    pe.wait_ge(s_xnT, j + 1)
                    nc.tensor.matmul(down_ps[:, 0:DQ + DKV], xnT[:, j, :], w_a[:, WDOWN:WDOWN + DQ + DKV],
                                     start=True, stop=True).then_inc(s_down, 1)
                if stage == "down_turn":
                    pe.wait_ge(s_cn, j + 1)
                    nc.tensor.transpose(down_ps[0:DQ, CQ0:CQ0 + D], cn[:, j, 0:DQ], ident[:, :]).then_inc(s_cqT_ps, 1)
                    wait_for(turn_read)
                    nc.tensor.transpose(turn_ps[0:DKV, 0:D], cn[:, j, DQ:], ident[:, :]).then_inc(s_ckvT_ps, 1)
                    turn_read = [(s_ckvT, j + 1)]
                if stage == "up":
                    pe.wait_ge(s_cqT, j + 1)
                    pe.wait_ge(s_xnT2, j + 1)
                    for par in range(2):
                        own = xnT2[:, j, par, :]
                        at = KR0 + par * HEADS * R
                        nc.tensor.matmul(down_ps[:, at:at + HEADS * R], own, w_a[:, WKR:WKR + HEADS * R],
                                         start=True, stop=True)
                    nc.tensor.matmul(down_ps[:, Q0:Q0 + HEADS * HD], cqT[:, j, :], w_q[:, 0:HEADS * HD],
                                     start=True, stop=True).then_inc(s_up_q, 1)
                    down_read = [(s_q_plain, j + 1), (s_q_rot, j + 1)]
                    pe.wait_ge(s_ckvT, j + 1)
                    if j:
                        pe.wait_ge(s_k, j)
                        pe.wait_ge(s_v, j)
                    for par in range(2):
                        own = ckvT[:, j, par, :]
                        mm = nc.tensor.matmul(kv_ps[:, par * 2 * D:(par + 1) * 2 * D], own, w_kv[:, 0:2 * D],
                                              start=True, stop=True)
                    mm.then_inc(s_up_kv, 1)
                if stage == "mix_turn":
                    wait_for(turn_read)
                    pe.wait_ge(s_on, j + 1)
                    nc.tensor.transpose(turn_ps[:, 0:D], on[:, j, :], ident[:, :]).then_inc(s_onT_ps, 1)
                    turn_read = [(s_onT, j + 1)]
                if stage == "attn_out":
                    wait_for(mm_read)
                    pe.wait_ge(s_onT, j + 1)
                    nc.tensor.matmul(mm_ps[:, 0:D], onT[:, j, :], w_a[:, WOUT:WOUT + D], start=True, stop=True) \
                        .then_inc(s_attn, 1)
                    mm_read = [(s_h2, j + 1)]
                if stage == "gru_in_turn":
                    wait_for(turn_read)
                    pe.wait_ge(s_xg, j + 1)
                    nc.tensor.transpose(turn_ps[:, 0:D], xg[:, j, :], ident[:, :]).then_inc(s_xgT_ps, 1)
                    turn_read = [(s_xgT, j + 1)]
                if stage == "gru":
                    t = j
                    if t == 0:
                        pe.wait_ge(s_wg, 16)
                        pe.wait_ge(s_scaled, 3)
                    gru_inputs(t)
                    for kc in range(KC) if t else ():
                        pe.wait_ge(s_hs[kc], t)
                        for m in range(KC):
                            mm = nc.tensor.matmul(rz_ps[m][:, 0:B], w_h(RG, kc, m), hs[:, kc, t - 1, :], start=False,
                                                  stop=(kc == KC - 1), skip_group_check=True)
                            if kc == KC - 1:
                                mm.then_inc(s_r_ps[m], 1)
                    for m in range(KC):
                        if t:
                            pe.wait_ge(s_tc[m], t)
                        mm = nc.tensor.matmul(c_ps[m][:, 0:B], w_x(CG, m), xgT[:, t, :], start=True, stop=(t == 0))
                        if t == 0:
                            mm.then_inc(s_c_ps[m], 1)
                    if t:
                        for m in range(KC):
                            pe.wait_ge(s_tr[m], t)
                            for kc in range(KC):
                                mm = nc.tensor.matmul(rz_ps[m][:, B:2 * B], w_h(ZG, kc, m), hs[:, kc, t - 1, :],
                                                      start=False, stop=(kc == KC - 1), skip_group_check=True)
                            mm.then_inc(s_z_ps[m], 1)
                        for kc in range(KC):
                            pe.wait_ge(s_rh[kc], t)
                            for m in range(KC):
                                mm = nc.tensor.matmul(c_ps[m][:, 0:B], w_h(CG, kc, m), rh[:, kc, :], start=False,
                                                      stop=(kc == KC - 1))
                                if kc == KC - 1:
                                    mm.then_inc(s_c_ps[m], 1)
                if stage == "out":
                    wait_for(mm_read)
                    nc.tensor.matmul(mm_ps[:, 0:D], ones[:, :], row_b[:, D:2 * D], start=True, stop=False)
                    for kc in range(KC):
                        pe.wait_ge(s_hs[kc], 2 * j + 2)
                        both = hs[:, kc, 2 * j:2 * j + 2, :].rearrange("p s b -> p (s b)")
                        mm = nc.tensor.matmul(mm_ps[:, 0:D], both, w_o(kc), start=False, stop=(kc == KC - 1))
                    mm.then_inc(s_out_ps, 1)
                    mm_read = [(s_ot, j + 1)]


def kernel(**inputs):
    import concourse.bacc as bacc
    from concourse.bass_utils import run_bass_kernel_spmd

    a = {n: np.asarray(w) for n, w in inputs.items()}

    def chunks(w):
        return w.reshape(-1, 128, w.shape[1]).transpose(1, 0, 2).reshape(128, -1)

    def per_head(plain, rotated):
        n = plain.shape[0]
        return np.concatenate([plain.reshape(n, HEADS, DH), rotated.reshape(n, HEADS, R)], 2).reshape(n, -1)

    f, g = "L0_attn_", "L0_ffn_"
    pack_a = np.concatenate([chunks(a["L0_tok_W"]), a[f + "W_dq"], a[f + "W_dkv"], a[f + "W_kr"], a[f + "W_o"].T], 1)
    pack_q = np.concatenate([per_head(a[f + "W_uq"], a[f + "W_qr"]), a[f + "q_ln_g"][:, None],
                             a[f + "q_ln_b"][:, None]], 1)
    pack_kv = np.concatenate([a[f + "W_ukv"], a[f + "kv_ln_g"][:, None], a[f + "kv_ln_b"][:, None]], 1)
    rows = np.stack([np.concatenate([a["L0_tok_b"], a[g + "bo"]]),
                     np.concatenate([a["L0_tok_gamma"], a["L0_tok_beta"]])])
    pack_g = np.concatenate([a[g + n].T for n in ("Wur", "Wuz", "Wu")] +
                            [chunks(a[g + n].T) for n in ("Wwr", "Wwz", "Ww", "Wo")] +
                            [chunks(a[g + n][:, None]) for n in ("bur", "buz", "bu", "bwr", "bwz", "bw")], 1)
    time = np.arange(T, dtype=np.float32)
    cos = np.repeat(np.cos(time)[:, None], HEADS * R, 1)
    sin = np.sin(time)[:, None] * np.tile(np.array([-1, 1], np.float32), HEADS)
    rot = np.stack([cos, sin], 1).reshape(NT, 2, 2, HEADS * R).astype(np.float32)
    rope_q = np.repeat(rot.transpose(1, 0, 2, 3), B, 0)
    rope_k = np.broadcast_to(rot.transpose(0, 2, 1, 3)[None], (128, NT, 2, 2, HEADS * R))
    arrays = {"x": a["x"].reshape(B, -1), "pack_a": pack_a, "pack_q": pack_q, "pack_kv": pack_kv, "rows": rows,
              "pack_g": pack_g, "rope_q": rope_q, "rope_k": rope_k}
    arrays = {n: np.ascontiguousarray(w) for n, w in arrays.items()}
    nc = bacc.Bacc("TRN2", target_bir_lowering=False, num_devices=1)
    args = [nc.dram_tensor(n, w.shape, mybir.dt.from_np(w.dtype), kind="ExternalInput").ap() for n, w in arrays.items()]
    out = nc.dram_tensor("out", (B, T, D), F32, kind="ExternalOutput").ap()
    audio_tower(nc, *args, out)
    r = run_bass_kernel_spmd(nc, [arrays], core_ids=[0])
    return r.results[0]["out"]
```

```python
from contextlib import ExitStack

import numpy as np

import concourse.bass as bass
from concourse import mybir

F32 = mybir.dt.float32
BF16 = mybir.dt.bfloat16
ALU = mybir.AluOpType
ACT = mybir.ActivationFunctionType
AX_X = mybir.AxisListType.X

B = 64
T = 10
NT = T // 2
D = 128
PATCH = 256
HEADS, DH, R = 8, 16, 2
HD = DH + R
DQ, DKV = D // 2, 2 * D // 3
H = 256
KC = H // 128
SCALE = float(HD) ** -0.5
LOWEST = float(np.finfo(np.float32).min)
EPS_TOK, EPS = 1e-3, 1e-5

TOKW = 0
WDOWN = TOKW + 2 * D
WKR = WDOWN + DQ + DKV
WOUT = WKR + HEADS * R
PACK_A = WOUT + D
WX = 0
WH = WX + 3 * H
WO = WH + 3 * KC * H
BIAS_X = WO + KC * D
BIAS_H = BIAS_X + 3 * KC
PACK_G = BIAS_H + 3 * KC
RG, ZG, CG = range(3)
UPQ = D + HEADS * R + 2 * HEADS * R
ROT = UPQ - D
LATENT = DQ + DKV

GROUPS = [[0], [1, 2], [3, 4]]
GROUP_STAGES = ("proj", "stats_tok", "norm_tok", "stats_pre", "norm_pre", "x_norm_turn", "down", "stats_down",
                "norm_down", "down_turn", "up_q")
PART = 3


def parts(j):
    S = 2 * j + 2
    n = -(-S // PART)
    return [(S * i // n, S * (i + 1) // n) for i in range(n)]


ORDER = [
    ("x_turn", 0), ("proj", 0), ("stats_tok", 0), ("norm_tok", 0), ("x_turn", 1), ("stats_pre", 0),
    ("norm_pre", 0), ("proj", 1), ("stats_tok", 1), ("x_norm_turn", 0), ("down", 0), ("stats_down", 0),
    ("norm_tok", 1), ("norm_down", 0), ("down_turn", 0), ("stats_pre", 1), ("up_q", 0), ("norm_pre", 1),
    ("up_kv", 0), ("x_norm_turn", 1), ("prod", 0, 0), ("down", 1), ("reduce", 0, 0), ("stats_down", 1),
    ("proj", 2), ("softmax", 0), ("stats_tok", 2), ("scale_weights", 0), ("norm_down", 1), ("weigh", 0),
    ("mix", 0, 0), ("norm_tok", 2), ("mix", 0, 1), ("mix_norm", 0), ("mix_turn", 0), ("attn_out", 0),
    ("down_turn", 1), ("stats_gru", 0), ("norm_gru", 0), ("up_q", 1), ("gru_in_turn", 0), ("up_kv", 1),
    ("gate_bias", 0), ("gru_x", 0), ("prod", 1, 0), ("stats_pre", 2), ("gru_x_candidate", 0), ("gru_x_update", 0),
    ("scale_weights", 1), ("gru_reset", 0), ("prod", 1, 1), ("reduce", 1, 1), ("reduce", 1, 0), ("gru_update", 0),
    ("softmax", 1), ("weigh", 1), ("gru_candidate", 0), ("up_kv", 2), ("norm_pre", 2), ("prod", 2, 0),
    ("mix", 1, 0), ("mix", 1, 1), ("mix_norm", 1), ("prod", 2, 1), ("gru_reset", 1), ("mix_turn", 1),
    ("attn_out", 1), ("reduce", 2, 1), ("scale_weights", 2), ("stats_gru", 1), ("reduce", 2, 0), ("gru_update", 1),
    ("x_norm_turn", 2), ("norm_gru", 1), ("gru_candidate", 1), ("gru_in_turn", 1), ("down", 2), ("stats_down", 2),
    ("gru_x", 1), ("softmax", 2), ("gru_reset", 2), ("norm_down", 2), ("weigh", 2), ("out", 0),
    ("gru_x_update", 1), ("gru_update", 2), ("gru_x_candidate", 1), ("mix", 2, 0), ("mix", 2, 1), ("down_turn", 2),
    ("up_q", 2), ("up_kv", 3), ("mix_norm", 2), ("prod", 3, 0), ("gru_candidate", 2), ("prod", 3, 1), ("up_kv", 4),
    ("mix_turn", 2), ("prod", 3, 2), ("reduce", 3, 1), ("gru_reset", 3), ("attn_out", 2), ("stats_gru", 2),
    ("reduce", 3, 2), ("reduce", 3, 0), ("gru_update", 3), ("prod", 4, 0), ("norm_gru", 2), ("softmax", 3),
    ("prod", 4, 1), ("gru_candidate", 3), ("prod", 4, 2), ("weigh", 3), ("prod", 4, 3), ("gru_in_turn", 2),
    ("reduce", 4, 1), ("gru_x", 2), ("mix", 3, 0), ("gru_reset", 4), ("gru_x_update", 2), ("mix", 3, 1),
    ("gru_update", 4), ("mix_norm", 3), ("reduce", 4, 2), ("gru_x_candidate", 2), ("gru_candidate", 4),
    ("mix_turn", 3), ("attn_out", 3), ("stats_gru", 3), ("reduce", 4, 3), ("reduce", 4, 0), ("gru_reset", 5),
    ("norm_gru", 3), ("softmax", 4), ("out", 1), ("gru_update", 5), ("gru_in_turn", 3), ("gru_candidate", 5),
    ("gru_x", 3), ("weigh", 4), ("mix", 4, 0), ("gru_x_update", 3), ("gru_reset", 6), ("mix", 4, 1),
    ("mix_norm", 4), ("gru_x_candidate", 3), ("gru_update", 6), ("gru_candidate", 6), ("mix_turn", 4), ("out", 2),
    ("attn_out", 4), ("stats_gru", 4), ("gru_reset", 7), ("norm_gru", 4), ("gru_update", 7), ("gru_candidate", 7),
    ("gru_in_turn", 4), ("gru_x", 4), ("gru_reset", 8), ("gru_x_candidate", 4), ("gru_x_update", 4),
    ("gru_update", 8), ("gru_candidate", 8), ("out", 3), ("gru_reset", 9), ("gru_update", 9), ("gru_candidate", 9),
    ("out", 4),
]
KEEP = (0, {
    ("x_turn", 0): 6, ("proj", 0): 2, ("x_turn", 1): 1, ("stats_pre", 0): 1, ("proj", 1): 6, ("stats_tok", 1): 2,
    ("x_norm_turn", 0): 1, ("down", 0): 2, ("norm_tok", 1): 8, ("stats_pre", 1): 1, ("up_kv", 0): 2,
    ("prod", 0, 0): 9, ("down", 1): 1, ("reduce", 0, 0): 1, ("weigh", 0): 5, ("mix", 0, 0): 14, ("mix", 0, 1): 2,
    ("mix_norm", 0): 2, ("mix_turn", 0): 3, ("attn_out", 0): 1, ("gru_in_turn", 0): 2,
})
FILL = (9, 2, 2, 11, 3, 1, 0, 1, 0)


def audio_tower(nc, x, pack_a, pack_q, pack_kv, rows, pack_g, rope, out):
    with ExitStack() as ctx:
        def sb(name, shape, dt=F32):
            return ctx.enter_context(nc.sbuf_tensor(name, shape, dt))

        def bank(name):
            return ctx.enter_context(nc.psum_tensor(name, [128, 512], F32))

        def sem(name):
            return ctx.enter_context(nc.semaphore(name))

        w_a = sb("w_a", [128, PACK_A])
        w_q = sb("w_q", [DQ, D + HEADS * R + 2])
        w_kv = sb("w_kv", [DKV, 2 * D + 2])
        w_g = sb("w_g", [128, PACK_G])
        w_hs = sb("w_hs", [128, 3 * KC * H + KC * D])
        half_bias = sb("half_bias", [128, 3 * KC])
        row_b = sb("row_b", [1, 2 * D])
        gamma_b = sb("gamma_b", [128, 2 * D])
        cs = sb("cs", [128, NT, 2, ROT])
        ident = sb("ident", [128, 128])
        ones = sb("ones", [1, 128])
        minus_half = sb("minus_half", [128, 8])
        zeros = sb("zeros", [128, 512], BF16)
        warm = sb("warm", [128, 1])
        x_sb = sb("x_sb", [B, (T + 1) * D])
        xT = sb("xT", [128, (T + 1) * B])
        hn = sb("hn", [128, NT, D])
        hg = sb("hg", [128, NT, D])
        h1 = sb("h1", [128, NT, D])
        xn = sb("xn", [128, NT, D])
        xnT = sb("xnT", [128, NT, D])
        xnT2 = sb("xnT2", [128, NT, 2, 2 * B])
        ckvT = sb("ckvT", [DKV, NT, 2, 2 * B])
        cn = sb("cn", [128, NT, LATENT])
        cqT = sb("cqT", [DQ, NT, D])
        q = sb("q", [128, NT, HEADS, HD])
        k = sb("k", [128, T, HEADS, HD])
        v = sb("v", [128, T, HEADS, DH])
        rot = sb("rot", [128, NT, ROT])
        rot_cos = sb("rot_cos", [128, NT, ROT])
        rot_sin = sb("rot_sin", [128, NT, ROT])
        prod = sb("prod", [128, T, HEADS, HD])
        sc = sb("sc", [128, T, HEADS])
        scm = sb("scm", [128, T, HEADS])
        p = sb("p", [128, T, HEADS])
        mx = sb("mx", [128, HEADS])
        den = sb("den", [128, HEADS])
        rden = sb("rden", [128, HEADS])
        prod_v = sb("prod_v", [128, T, HEADS, DH])
        mixed = sb("mixed", [128, D])
        on = sb("on", [128, NT, D])
        onT = sb("onT", [128, NT, D])
        h2h = sb("h2h", [128, NT, D])
        xg = sb("xg", [128, NT, D])
        xgT = sb("xgT", [128, T, B])
        stats = sb("stats", [128, NT, 5, 6])
        mv = sb("mv", [128, NT, 5, 2])
        ve = sb("ve", [128, 5, NT])
        rstd = sb("rstd", [128, 5, NT])
        shift = sb("shift", [128, 5, NT])
        hs = sb("hs", [128, KC, T, B])
        tr = sb("tr", [128, KC, B])
        tz = sb("tz", [128, KC, B])
        tc = sb("tc", [128, KC, B])
        rh = sb("rh", [128, KC, B])
        keep = sb("keep", [128, KC, B])
        move = sb("move", [128, KC, B])
        ot = sb("ot", [128, NT, D])
        o = sb("o", [128, NT, D])

        turn_ps = bank("turn_ps")
        mm_ps = bank("mm_ps")
        kv_ps = bank("kv_ps")
        r_ps = [bank(f"r_ps{m}") for m in range(KC)]
        z_ps = bank("z_ps")
        c_ps = [bank(f"c_ps{m}") for m in range(KC)]

        s_x = sem("s_x")
        s_wa = sem("s_wa")
        s_wq = sem("s_wq")
        s_wkv = sem("s_wkv")
        s_rows = sem("s_rows")
        s_gamma = sem("s_gamma")
        s_rope = sem("s_rope")
        s_wg = sem("s_wg")
        s_const = sem("s_const")
        s_zeros = sem("s_zeros")
        s_warm = sem("s_warm")
        s_ident = sem("s_ident")
        s_scaled = sem("s_scaled")
        s_hbias = sem("s_hbias")
        s_xT_ps = sem("s_xT_ps")
        s_xT = sem("s_xT")
        s_proj = sem("s_proj")
        NORMS = ("tok", "pre", "down", "gru")
        s_stats = {n: sem(f"s_stats_{n}") for n in NORMS}
        s_mv = {n: sem(f"s_mv_{n}") for n in NORMS}
        s_ve = {n: sem(f"s_ve_{n}") for n in NORMS}
        s_rstd = {n: sem(f"s_rstd_{n}") for n in NORMS}
        s_shift = {n: sem(f"s_shift_{n}") for n in NORMS}
        s_hn = sem("s_hn")
        s_hg = sem("s_hg")
        s_h1 = sem("s_h1")
        s_xn = sem("s_xn")
        s_xnT_ps = sem("s_xnT_ps")
        s_xnT = sem("s_xnT")
        s_xnT2 = sem("s_xnT2")
        s_down = sem("s_down")
        s_cn = sem("s_cn")
        s_cT_ps = sem("s_cT_ps")
        s_cqT = sem("s_cqT")
        s_ckvT = sem("s_ckvT")
        s_up_q = sem("s_up_q")
        s_up_kv = sem("s_up_kv")
        s_rot = sem("s_rot")
        s_q_plain = sem("s_q_plain")
        s_rot_parts = sem("s_rot_parts")
        s_q_rot = sem("s_q_rot")
        s_k_rot = sem("s_k_rot")
        s_k = sem("s_k")
        s_v = sem("s_v")
        s_prod = sem("s_prod")
        s_prod_pool = sem("s_prod_pool")
        s_sc = sem("s_sc")
        s_masked = sem("s_masked")
        s_mx = sem("s_mx")
        s_scm = sem("s_scm")
        s_p = sem("s_p")
        s_den = sem("s_den")
        s_rden = sem("s_rden")
        s_prod_v = sem("s_prod_v")
        s_mixed = sem("s_mixed")
        s_on = sem("s_on")
        s_onT_ps = sem("s_onT_ps")
        s_onT = sem("s_onT")
        s_h2_ps = sem("s_h2_ps")
        s_h2h = sem("s_h2h")
        s_xg = sem("s_xg")
        s_xgT_ps = sem("s_xgT_ps")
        s_xgT = sem("s_xgT")
        s_r_ps = [sem(f"s_r_ps{m}") for m in range(KC)]
        s_z_ps = sem("s_z_ps")
        s_c_ps = [sem(f"s_c_ps{m}") for m in range(KC)]
        s_tr = [sem(f"s_tr{m}") for m in range(KC)]
        s_tz = [sem(f"s_tz{m}") for m in range(KC)]
        s_tc = [sem(f"s_tc{m}") for m in range(KC)]
        s_rh = [sem(f"s_rh{m}") for m in range(KC)]
        s_keep = sem("s_keep")
        s_move = [sem(f"s_move{m}") for m in range(KC)]
        s_hs = [sem(f"s_hs{m}") for m in range(KC)]
        s_out_ps = sem("s_out_ps")
        s_ot = sem("s_ot")
        s_o = sem("s_o")
        s_stored = sem("s_stored")

        block = ctx.enter_context(nc.Block())

        def w_x(g, m):
            return w_g[:, WX + g * H + m * 128:WX + g * H + (m + 1) * 128]

        def w_h(g, kc, m):
            at = (g * KC + kc) * H + m * 128
            return w_hs[:, at:at + 128]

        def w_o(kc):
            at = 3 * KC * H + kc * D
            return w_hs[:, at:at + D]

        def r_cols(m, t):
            return r_ps[m][:, (t % 2) * B:(t % 2 + 1) * B]

        def z_cols(m, t):
            return z_ps[:, (2 * m + t % 2) * B:(2 * m + t % 2 + 1) * B]

        def c_cols(m, t):
            return c_ps[m][:, (t % 2) * B:(t % 2 + 1) * B]

        def parts_done(j):
            return sum(len(parts(i)) for i in range(j))

        def tiles_done(g):
            return GROUPS[g][-1] + 1

        def affine_tok(eng, nc_eng, g):
            a, b = GROUPS[g][0], tiles_done(g)
            gains = gamma_b[:, 0:D].unsqueeze(1).broadcast_to([128, b - a, D])
            shifts = gamma_b[:, D:2 * D].unsqueeze(1).broadcast_to([128, b - a, D])
            eng.wait_ge(s_hn, b)
            eng.wait_ge(s_gamma, 16)
            nc_eng.tensor_tensor(hg[:, a:b, :], hn[:, a:b, :], gains, ALU.mult).then_inc(s_hg, 1)
            eng.wait_ge(s_hg, g + 1)
            nc_eng.tensor_tensor(h1[:, a:b, :], hg[:, a:b, :], shifts, ALU.add).then_inc(s_h1, 1)

        def query_key_products(eng, nc_eng, j, i):
            lo, hi = parts(j)[i]
            eng.wait_ge(s_q_rot, j + 1)
            eng.wait_ge(s_q_plain, j + 1)
            eng.wait_ge(s_k_rot, j + 1)
            eng.wait_ge(s_k, j + 1)
            flat = "p s h d -> p s (h d)"
            queries = q[:, j:j + 1, :, :].rearrange(flat).broadcast_to([128, hi - lo, HEADS * HD])
            return nc_eng.tensor_tensor(prod[:, lo:hi, :, :].rearrange(flat), k[:, lo:hi, :, :].rearrange(flat),
                                        queries, ALU.mult)

        def weighted_values(eng, nc_eng, j):
            S = 2 * j + 2
            eng.wait_ge(s_p, j + 1)
            eng.wait_ge(s_v, j + 1)
            if j:
                eng.wait_ge(s_mixed, 2 * j)
            weights = p[:, 0:S, :].rearrange("p s h -> p (s h)").unsqueeze(2).broadcast_to([128, S * HEADS, DH])
            nc_eng.tensor_tensor(prod_v[:, 0:S, :, :].rearrange("p s h d -> p (s h) d"),
                                 v[:, 0:S, :, :].rearrange("p s h d -> p (s h) d"), weights, ALU.mult) \
                .then_inc(s_prod_v, 1)

        @block.sync
        def _(sp):
            sp.dma_start(x_sb[:, :], x[:, 0:(T + 1) * D]).then_inc(s_x, 16)
            sp.dma_start(gamma_b[:, :], rows[1:2, :].broadcast_to([128, 2 * D])).then_inc(s_gamma, 16)
            sp.dma_start(w_kv[:, :], pack_kv).then_inc(s_wkv, 16)
            sp.dma_start(w_g[:, :], pack_g).then_inc(s_wg, 16)
            for stage, j, *_ in ORDER:
                if stage == "out":
                    sp.wait_ge(s_o, j + 1)
                    for par in range(2):
                        sp.dma_start(out[:, 2 * j + par, :], o[par * B:(par + 1) * B, j, :]).then_inc(s_stored, 16)
            sp.wait_ge(s_stored, 16 * T)

        @block.gpsimd
        def _(pool):
            nc.gpsimd.memset(warm[:, :], 0.0).then_inc(s_warm, 1)
            nc.gpsimd.memset(ident[:, :], 0.0).then_inc(s_const, 1)
            nc.gpsimd.memset(ones[:, :], 1.0).then_inc(s_const, 1)
            nc.gpsimd.memset(minus_half[:, :], -0.5).then_inc(s_const, 1)
            pool.wait_ge(s_const, 3)
            nc.gpsimd.affine_select(out=ident[:, :], in_=ident[:, :], compare_op=ALU.not_equal, fill=1.0, base=0,
                                    pattern=[[-1, 128]], channel_multiplier=1).then_inc(s_ident, 1)

            def group_power(name, at, n, g, eps):
                a, b = GROUPS[g][0], GROUPS[g][-1] + 1
                pool.wait_ge(s_mv[name], n * b)
                nc.gpsimd.tensor_scalar(ve[:, at:at + n, a:b], mv[:, a:b, at:at + n, 1].rearrange("p j n -> p n j"),
                                        1.0, eps, ALU.mult, ALU.add).then_inc(s_ve[name], 1)
                pool.wait_ge(s_ve[name], g + 1)
                half = minus_half[:, 0:n * (b - a)].rearrange("p (n j) -> p n j", n=n)
                nc.gpsimd.tensor_tensor(rstd[:, at:at + n, a:b], ve[:, at:at + n, a:b], half,
                                        ALU.pow).then_inc(s_rstd[name], 1)

            for stage, j, *part in ORDER:
                a, b = (GROUPS[j][0], GROUPS[j][-1] + 1) if stage in GROUP_STAGES else (j, j + 1)
                if stage == "stats_tok":
                    group_power("tok", 0, 1, j, EPS_TOK)
                if stage == "stats_pre":
                    group_power("pre", 1, 1, j, EPS)
                if stage == "stats_down":
                    group_power("down", 2, 2, j, EPS)
                if stage == "norm_tok" and j == len(GROUPS) - 1:
                    affine_tok(pool, nc.gpsimd, j)
                if stage == "scale_weights":
                    lo, hi, factor = ((0, 2 * KC * H, 0.5), (2 * KC * H, 3 * KC * H, 0.25),
                                      (3 * KC * H, 3 * KC * H + KC * D, 0.5))[j]
                    pool.wait_ge(s_wg, 16)
                    nc.gpsimd.tensor_scalar(w_hs[:, lo:hi], w_g[:, WH + lo:WH + hi], factor, 1.0, ALU.mult,
                                            ALU.mult).then_inc(s_scaled, 1)
                if stage == "up_q":
                    pool.wait_ge(s_rot, j + 1)
                    if j == 0:
                        pool.wait_ge(s_rope, 16)
                    nc.gpsimd.tensor_tensor(rot_cos[:, a:b, :], rot[:, a:b, :], cs[:, a:b, 0, :], ALU.mult) \
                        .then_inc(s_rot_parts, 1)
                    pairs = "p j (h r) -> p (j h) r"
                    sins = cs[:, a:b, 1, :].rearrange("p j (h r) -> p j h r", r=R)
                    rots = rot[:, a:b, :].rearrange("p j (h r) -> p j h r", r=R)
                    dst = rot_sin[:, a:b, :].rearrange("p j (h r) -> p j h r", r=R)
                    for r in range(R):
                        nc.gpsimd.tensor_tensor(dst[:, :, :, r], rots[:, :, :, 1 - r], sins[:, :, :, r], ALU.mult) \
                            .then_inc(s_rot_parts, 1)
                    pool.wait_ge(s_rot_parts, 3 * (j + 1))
                    qr = HEADS * R
                    for i in range(a, b):
                        cos_i, sin_i = rot_cos[:, i, :], rot_sin[:, i, :]
                        nc.gpsimd.tensor_tensor(q[:, i, :, DH:HD], cos_i[:, 0:qr].rearrange("p (h r) -> p h r", r=R),
                                                sin_i[:, 0:qr].rearrange("p (h r) -> p h r", r=R), ALU.add) \
                            .then_inc(s_q_rot, 1)
                        nc.gpsimd.tensor_tensor(k[:, 2 * i:2 * i + 2, :, DH:HD],
                                                cos_i[:, qr:].rearrange("p (s h r) -> p s h r", s=2, r=R),
                                                sin_i[:, qr:].rearrange("p (s h r) -> p s h r", s=2, r=R), ALU.add) \
                            .then_inc(s_k_rot, 1)
                if stage == "prod" and len(parts(j)) > 1 and part[0] == 0:
                    pool.wait_ge(s_sc, parts_done(j))
                    query_key_products(pool, nc.gpsimd, j, 0).then_inc(s_prod_pool, 1)
                if stage == "weigh" and j:
                    weighted_values(pool, nc.gpsimd, j)
                if stage == "stats_gru":
                    pool.wait_ge(s_mv["gru"], j + 1)
                    nc.gpsimd.tensor_scalar(ve[:, 4, j:j + 1], mv[:, j, 4, 1:2], 1.0, EPS, ALU.mult, ALU.add) \
                        .then_inc(s_ve["gru"], 1)
                    pool.wait_ge(s_ve["gru"], j + 1)
                    nc.gpsimd.tensor_tensor(rstd[:, 4, j:j + 1], ve[:, 4, j:j + 1], minus_half[:, 0:1], ALU.pow) \
                        .then_inc(s_rstd["gru"], 1)

        @block.scalar
        def _(act):
            act.dma_start(w_a[:, :], pack_a).then_inc(s_wa, 16)
            act.wait_ge(s_warm, 1)
            nc.scalar.activation(warm[:, :], warm[:, :], ACT.Tanh)
            act.dma_start(row_b[:, :], rows[0:1, :]).then_inc(s_rows, 16)
            act.dma_start(w_q[:, :], pack_q).then_inc(s_wq, 16)
            act.dma_start(cs[:, :, :, :], rope).then_inc(s_rope, 16)

            def shifted(dst, src, j, at):
                return nc.scalar.activation(dst, src, ACT.Identity, bias=shift[:, at, j:j + 1],
                                            scale=rstd[:, at, j:j + 1])

            for stage, j, *_ in ORDER:
                a, b = (GROUPS[j][0], GROUPS[j][-1] + 1) if stage in GROUP_STAGES else (j, j + 1)
                n = b - a
                if stage == "norm_tok" and j:
                    act.wait_ge(s_shift["tok"], j)
                    for i in range(n):
                        shifted(hn[:, a + i, :], mm_ps[:, i * D:(i + 1) * D], a + i, 0).then_inc(s_hn, 1)
                if stage == "norm_pre" and j:
                    act.wait_ge(s_shift["pre"], j)
                    for i in range(a, b):
                        shifted(xn[:, i, :], h1[:, i, :], i, 1).then_inc(s_xn, 1)
                if stage == "norm_down" and j:
                    act.wait_ge(s_shift["down"], j)
                    for i in range(n):
                        for s, c, d in ((2, 0, DQ), (3, DQ, LATENT)):
                            shifted(cn[:, a + i, c:d], kv_ps[:, i * LATENT + c:i * LATENT + d], a + i, s) \
                                .then_inc(s_cn, 1)
                if stage == "norm_gru" and j:
                    act.wait_ge(s_shift["gru"], j)
                    shifted(xg[:, j, :], kv_ps[:, 0:D], j, 4).then_inc(s_xg, 1)
                if stage == "x_turn":
                    act.wait_ge(s_xT_ps, j + 1)
                    if j == 0:
                        nc.scalar.copy(xT[:, 0:3 * B], turn_ps[:, 0:3 * B]).then_inc(s_xT, 1)
                    else:
                        nc.scalar.copy(xT[:, 3 * B:], kv_ps[:, 0:(T - 2) * B]).then_inc(s_xT, 1)
                if stage == "x_norm_turn":
                    act.wait_ge(s_xnT_ps, j + 1)
                    nc.scalar.copy(xnT[:, a:b, :].rearrange("p j c -> p (j c)"), turn_ps[:, 0:n * D]).then_inc(s_xnT, 1)
                    nc.scalar.copy(xnT2[:, a:b, :, :].rearrange("p j s (e b) -> p (j s) e b", e=2),
                                   turn_ps[:, 0:n * D].rearrange("p (s b) -> p s b", b=B).unsqueeze(2)
                                   .broadcast_to([128, 2 * n, 2, B])).then_inc(s_xnT2, 1)
                if stage == "down_turn":
                    act.wait_ge(s_cT_ps, j + 1)
                    if j == 0:
                        act.wait_ge(s_wq, 16)
                        act.wait_ge(s_wkv, 16)
                    nc.scalar.activation(cqT[:, a:b, :].rearrange("p j c -> p (j c)"), turn_ps[0:DQ, 0:n * D],
                                         ACT.Identity, bias=w_q[:, D + HEADS * R + 1:D + HEADS * R + 2],
                                         scale=w_q[:, D + HEADS * R:D + HEADS * R + 1]).then_inc(s_cqT, 1)
                    nc.scalar.activation(ckvT[:, a:b, :, :].rearrange("p j s (e b) -> p (j s) e b", e=2),
                                         turn_ps[0:DKV, n * D:2 * n * D].rearrange("p (s b) -> p s b", b=B)
                                         .unsqueeze(2).broadcast_to([DKV, 2 * n, 2, B]), ACT.Identity,
                                         bias=w_kv[:, 2 * D + 1:2 * D + 2], scale=w_kv[:, 2 * D:2 * D + 1]) \
                        .then_inc(s_ckvT, 1)
                if stage == "up_q":
                    act.wait_ge(s_up_q, j + 1)
                    up = mm_ps[:, 0:n * UPQ].rearrange("p (j c) -> p j c", j=n)
                    nc.scalar.copy(rot[:, a:b, :], up[:, :, D:UPQ]).then_inc(s_rot, 1)
                    for i in range(n):
                        nc.scalar.copy(q[:, a + i, :, 0:DH], up[:, i, 0:D].rearrange("p (h d) -> p h d", h=HEADS)) \
                            .then_inc(s_q_plain, 1)
                if stage == "up_kv":
                    act.wait_ge(s_up_kv, j + 1)
                    kv = kv_ps[:, :].rearrange("p (s e h d) -> p s e h d", s=2, e=2, h=HEADS)
                    nc.scalar.copy(k[:, 2 * j:2 * j + 2, :, 0:DH], kv[:, :, 0, :, :]).then_inc(s_k, 1)
                    nc.scalar.copy(v[:, 2 * j:2 * j + 2, :, :], kv[:, :, 1, :, :]).then_inc(s_v, 1)
                if stage == "softmax":
                    act.wait_ge(s_scm, j + 1)
                    if j:
                        act.wait_ge(s_prod_v, j)
                        act.wait_ge(s_den, j)
                    S = 2 * j + 2
                    nc.scalar.activation(p[:, 0:S, :], scm[:, 0:S, :], ACT.Exp, scale=SCALE).then_inc(s_p, 1)
                if stage == "mix_turn":
                    act.wait_ge(s_onT_ps, j + 1)
                    nc.scalar.copy(onT[:, j, :], turn_ps[:, 0:D]).then_inc(s_onT, 1)
                if stage == "stats_gru":
                    act.wait_ge(s_stats["gru"], j + 1)
                    nc.scalar.activation(h2h[:, j, :], kv_ps[:, 0:D], ACT.Copy, bias=0.5).then_inc(s_h2h, 1)
                if stage == "gru_in_turn":
                    act.wait_ge(s_xgT_ps, j + 1)
                    nc.scalar.copy(xgT[:, 2 * j:2 * j + 2, :],
                                   turn_ps[:, 0:D].rearrange("p (s b) -> p s b", s=2)).then_inc(s_xgT, 1)
                t = j
                if stage == "gru_reset" and t:
                    for m in range(KC):
                        act.wait_ge(s_r_ps[m], t)
                        nc.scalar.activation(tr[:, m, :], r_cols(m, t), ACT.Tanh, scale=0.5,
                                             bias=half_bias[:, m:m + 1]).then_inc(s_tr[m], 1)
                if stage == "gru_update":
                    if t == 0:
                        act.wait_ge(s_hbias, 2)
                    act.wait_ge(s_z_ps, t + 1)
                    for m in range(KC):
                        nc.scalar.activation(tz[:, m, :], z_cols(m, t), ACT.Tanh, scale=0.5,
                                             bias=half_bias[:, KC + m:KC + m + 1]).then_inc(s_tz[m], 1)
                if stage == "gru_candidate":
                    for m in range(KC):
                        act.wait_ge(s_c_ps[m], t + 1)
                        nc.scalar.activation(tc[:, m, :], c_cols(m, t), ACT.Tanh,
                                             bias=half_bias[:, 2 * KC + m:2 * KC + m + 1]).then_inc(s_tc[m], 1)
                if stage == "out":
                    act.wait_ge(s_out_ps, j + 1)
                    nc.scalar.activation(ot[:, j, :], mm_ps[:, 0:D], ACT.Tanh, scale=0.5).then_inc(s_ot, 1)

        @block.vector
        def _(dve):
            nc.vector.memset(zeros[:, :], 0.0).then_inc(s_zeros, 1)
            stats_done = {n: 0 for n in NORMS}

            def moments(name, rows_):
                for j, at, src in rows_:
                    nc.vector.bn_stats(stats[:, j, at, :], src).then_inc(s_stats[name], 1)
                for j, at, src in rows_:
                    stats_done[name] += 1
                    dve.wait_ge(s_stats[name], stats_done[name])
                    nc.vector.bn_aggr(mv[:, j, at, :], stats[:, j, at, :]).then_inc(s_mv[name], 1)

            def normed(dst, src, j, at):
                return nc.vector.tensor_scalar(dst, src, mv[:, j, at, 0:1], rstd[:, at, j:j + 1], ALU.subtract,
                                               ALU.mult)

            def shifts(name, a, b, at, n):
                if a:
                    nc.vector.scalar_tensor_tensor(out=shift[:, at:at + n, a:b],
                                                   in0=mv[:, a:b, at:at + n, 0].rearrange("p j n -> p n j"),
                                                   scalar=-1.0, in1=rstd[:, at:at + n, a:b], op0=ALU.mult,
                                                   op1=ALU.mult).then_inc(s_shift[name], 1)

            for stage, j, *part in ORDER:
                a, b = (GROUPS[j][0], GROUPS[j][-1] + 1) if stage in GROUP_STAGES else (j, j + 1)
                n = b - a
                if stage == "stats_tok":
                    dve.wait_ge(s_proj, j + 1)
                    moments("tok", [(a + i, 0, mm_ps[:, i * D:(i + 1) * D]) for i in range(n)])
                if stage == "norm_tok":
                    dve.wait_ge(s_rstd["tok"], j + 1)
                    if j == 0:
                        normed(hn[:, 0, :], mm_ps[:, 0:D], 0, 0).then_inc(s_hn, 1)
                    shifts("tok", a, b, 0, 1)
                    if j < len(GROUPS) - 1:
                        affine_tok(dve, nc.vector, j)
                if stage == "stats_pre":
                    dve.wait_ge(s_h1, j + 1)
                    moments("pre", [(i, 1, h1[:, i, :]) for i in range(a, b)])
                if stage == "norm_pre":
                    dve.wait_ge(s_rstd["pre"], j + 1)
                    if j == 0:
                        normed(xn[:, 0, :], h1[:, 0, :], 0, 1).then_inc(s_xn, 1)
                    shifts("pre", a, b, 1, 1)
                if stage == "stats_down":
                    dve.wait_ge(s_down, j + 1)
                    moments("down", [(a + i, s, kv_ps[:, i * LATENT + c:i * LATENT + d])
                                     for i in range(n) for s, c, d in ((2, 0, DQ), (3, DQ, LATENT))])
                if stage == "norm_down":
                    dve.wait_ge(s_rstd["down"], j + 1)
                    for s, c, d in ((2, 0, DQ), (3, DQ, LATENT)) if j == 0 else ():
                        normed(cn[:, 0, c:d], kv_ps[:, c:d], 0, s).then_inc(s_cn, 1)
                    shifts("down", a, b, 2, 2)
                S = 2 * j + 2
                if stage == "prod" and (len(parts(j)) == 1 or part[0]):
                    query_key_products(dve, nc.vector, j, part[0]).then_inc(s_prod, 1)
                if stage == "reduce":
                    lo, hi = parts(j)[part[0]]
                    if len(parts(j)) > 1 and part[0] == 0:
                        dve.wait_ge(s_prod_pool, j)
                    else:
                        dve.wait_ge(s_prod, max(parts_done(j) - j, 0) + max(part[0], 1) + (j > 0))
                    nc.vector.tensor_reduce(sc[:, lo:hi, :], prod[:, lo:hi, :, :], AX_X, ALU.add).then_inc(s_sc, 1)
                if stage == "softmax":
                    dve.wait_ge(s_sc, parts_done(j + 1))
                    nc.vector.memset(sc[0:B, S - 1, :], LOWEST).then_inc(s_masked, 1)
                    dve.wait_ge(s_masked, j + 1)
                    nc.vector.tensor_reduce(mx[:, :], sc[:, 0:S, :].rearrange("p s h -> p h s"), AX_X, ALU.max) \
                        .then_inc(s_mx, 1)
                    dve.wait_ge(s_mx, j + 1)
                    if j:
                        dve.wait_ge(s_p, j)
                    nc.vector.tensor_tensor(scm[:, 0:S, :], sc[:, 0:S, :],
                                            mx[:, :].unsqueeze(1).broadcast_to([128, S, HEADS]), ALU.subtract) \
                        .then_inc(s_scm, 1)
                if stage == "weigh":
                    if j == 0:
                        weighted_values(dve, nc.vector, j)
                    dve.wait_ge(s_p, j + 1)
                    nc.vector.tensor_reduce(den[:, :], p[:, 0:S, :].rearrange("p s h -> p h s"), AX_X, ALU.add) \
                        .then_inc(s_den, 1)
                    dve.wait_ge(s_den, j + 1)
                    nc.vector.reciprocal(rden[:, :], den[:, :]).then_inc(s_rden, 1)
                if stage == "mix":
                    dve.wait_ge(s_prod_v, j + 1)
                    half = slice(part[0] * (D // 2), (part[0] + 1) * (D // 2))
                    nc.vector.tensor_reduce(mixed[:, half],
                                            prod_v[:, 0:S, :, :].rearrange("p s h d -> p (h d) s")[:, half, :], AX_X,
                                            ALU.add).then_inc(s_mixed, 1)
                if stage == "mix_norm":
                    dve.wait_ge(s_mixed, 2 * (j + 1))
                    dve.wait_ge(s_rden, j + 1)
                    nc.vector.tensor_tensor(on[:, j, :].rearrange("p (h d) -> p h d", h=HEADS),
                                            mixed[:, :].rearrange("p (h d) -> p h d", h=HEADS),
                                            rden[:, :].unsqueeze(2).broadcast_to([128, HEADS, DH]), ALU.mult) \
                        .then_inc(s_on, 1)
                if stage == "stats_gru":
                    dve.wait_ge(s_h2_ps, j + 1)
                    moments("gru", [(j, 4, kv_ps[:, 0:D])])
                if stage == "norm_gru":
                    dve.wait_ge(s_rstd["gru"], j + 1)
                    if j == 0:
                        dve.wait_ge(s_h2h, j + 1)
                        normed(xg[:, j, :], kv_ps[:, 0:D], j, 4).then_inc(s_xg, 1)
                    shifts("gru", a, b, 4, 1)
                t = j
                if stage == "gate_bias":
                    dve.wait_ge(s_wg, 16)
                    nc.vector.tensor_tensor(half_bias[:, :], w_g[:, BIAS_X:BIAS_X + 3 * KC],
                                            w_g[:, BIAS_H:BIAS_H + 3 * KC], ALU.add).then_inc(s_hbias, 1)
                    dve.wait_ge(s_hbias, 1)
                    nc.vector.tensor_scalar(half_bias[:, 0:2 * KC], half_bias[:, 0:2 * KC], 0.5, None,
                                            ALU.mult).then_inc(s_hbias, 1)
                if stage == "gru_reset":
                    for m in range(KC) if t else ():
                        dve.wait_ge(s_tr[m], t)
                        nc.vector.scalar_tensor_tensor(out=rh[:, m, :], in0=tr[:, m, :], scalar=1.0,
                                                       in1=hs[:, m, t - 1, :], op0=ALU.add, op1=ALU.mult) \
                            .then_inc(s_rh[m], 1)
                if stage == "gru_update" and t:
                    for m in range(KC):
                        dve.wait_ge(s_tz[m], t + 1)
                    nc.vector.scalar_tensor_tensor(out=keep[:, :, :], in0=tz[:, :, :], scalar=1.0,
                                                   in1=hs[:, :, t - 1, :], op0=ALU.add, op1=ALU.mult) \
                        .then_inc(s_keep, 1)
                if stage == "gru_candidate":
                    for m in range(KC):
                        dve.wait_ge(s_tc[m], t + 1)
                        nc.vector.scalar_tensor_tensor(out=move[:, m, :], in0=tz[:, m, :], scalar=1.0,
                                                       in1=tc[:, m, :], op0=ALU.subtract, op1=ALU.mult) \
                            .then_inc(s_move[m], 1)
                        dve.wait_ge(s_move[m], t + 1)
                        if t:
                            dve.wait_ge(s_keep, t)
                            nc.vector.scalar_tensor_tensor(out=hs[:, m, t, :], in0=keep[:, m, :], scalar=0.5,
                                                           in1=move[:, m, :], op0=ALU.mult, op1=ALU.subtract) \
                                .then_inc(s_hs[m], 1)
                        else:
                            nc.vector.tensor_scalar(hs[:, m, t, :], move[:, m, :], -1.0, None, ALU.mult) \
                                .then_inc(s_hs[m], 1)
                if stage == "out":
                    dve.wait_ge(s_ot, j + 1)
                    nc.vector.scalar_tensor_tensor(out=o[:, j, :], in0=ot[:, j, :], scalar=0.5, in1=h2h[:, j, :],
                                                   op0=ALU.mult, op1=ALU.add).then_inc(s_o, 1)

        @block.tensor
        def _(pe):
            turn_read, mm_read, kv_read = [], [], []

            def wait_for(read):
                for s, n in read:
                    pe.wait_ge(s, n)

            def keep_clock(n):
                for _ in range(n):
                    nc.tensor.matmul(c_ps[1][:, :], zeros[:, 0:128], zeros[:, :], start=True, stop=True)

            pe.wait_ge(s_zeros, 1)
            keep_clock(KEEP[0])
            pe.wait_ge(s_ident, 1)
            before_gru = True
            for stage, j, *_ in ORDER:
                a, b = (GROUPS[j][0], GROUPS[j][-1] + 1) if stage in GROUP_STAGES else (j, j + 1)
                n = b - a
                if stage == "gru_x" and j == 0:
                    before_gru = False
                if before_gru:
                    keep_clock(KEEP[1].get((stage, j), 0))
                if stage == "x_turn":
                    if j == 0:
                        pe.wait_ge(s_x, 16)
                    lo, hi, dst = (0, 3, turn_ps) if j == 0 else (3, T + 1, kv_ps)
                    for c in range(lo, hi):
                        mm = nc.tensor.transpose(dst[:, (c - lo) * B:(c - lo + 1) * B], x_sb[:, c * D:(c + 1) * D],
                                                 ident[0:B, 0:B])
                    mm.then_inc(s_xT_ps, 1)
                    if j == 0:
                        turn_read = [(s_xT, 1)]
                    else:
                        kv_read = [(s_xT, 2)]
                if stage == "proj":
                    wait_for(mm_read)
                    pe.wait_ge(s_xT, min(j + 1, 2))
                    if j == 0:
                        pe.wait_ge(s_wa, 16)
                    for i in range(n):
                        for e in range(2):
                            at = (2 * (a + i) + e) * B
                            nc.tensor.matmul(mm_ps[:, i * D:(i + 1) * D], xT[:, at:at + 2 * B],
                                             w_a[:, TOKW + e * D:TOKW + (e + 1) * D], start=(e == 0), stop=False)
                        if j == 0:
                            pe.wait_ge(s_rows, 16)
                            pe.wait_ge(s_const, 3)
                        mm = nc.tensor.matmul(mm_ps[:, i * D:(i + 1) * D], ones[:, :], row_b[:, 0:D], start=False,
                                              stop=True)
                    mm.then_inc(s_proj, 1)
                    mm_read = [(s_hn, b)]
                if stage == "x_norm_turn":
                    wait_for(turn_read)
                    for i in range(n):
                        pe.wait_ge(s_xn, a + i + 1)
                        mm = nc.tensor.transpose(turn_ps[:, i * D:(i + 1) * D], xn[:, a + i, :], ident[:, :])
                    mm.then_inc(s_xnT_ps, 1)
                    turn_read = [(s_xnT2, j + 1)]
                if stage == "down":
                    wait_for(kv_read)
                    pe.wait_ge(s_xnT, j + 1)
                    for i in range(n):
                        mm = nc.tensor.matmul(kv_ps[:, i * LATENT:(i + 1) * LATENT], xnT[:, a + i, :],
                                              w_a[:, WDOWN:WDOWN + LATENT], start=True, stop=True)
                    mm.then_inc(s_down, 1)
                    kv_read = [(s_cn, 2 * b)]
                if stage == "down_turn":
                    wait_for(turn_read)
                    for i in range(n):
                        pe.wait_ge(s_cn, 2 * (a + i) + 1)
                        nc.tensor.transpose(turn_ps[0:DQ, i * D:(i + 1) * D], cn[:, a + i, 0:DQ], ident[:, :])
                        pe.wait_ge(s_cn, 2 * (a + i) + 2)
                        mm = nc.tensor.transpose(turn_ps[0:DKV, (n + i) * D:(n + i + 1) * D], cn[:, a + i, DQ:],
                                                 ident[:, :])
                    mm.then_inc(s_cT_ps, 1)
                    turn_read = [(s_ckvT, j + 1)]
                if stage == "up_q":
                    wait_for(mm_read)
                    pe.wait_ge(s_xnT2, j + 1)
                    for i in range(n):
                        for par in range(2):
                            at = i * UPQ + D + (1 + par) * HEADS * R
                            nc.tensor.matmul(mm_ps[:, at:at + HEADS * R], xnT2[:, a + i, par, :],
                                             w_a[:, WKR:WKR + HEADS * R], start=True, stop=True)
                    pe.wait_ge(s_cqT, j + 1)
                    for i in range(n):
                        mm = nc.tensor.matmul(mm_ps[:, i * UPQ:i * UPQ + D + HEADS * R], cqT[:, a + i, :],
                                              w_q[:, 0:D + HEADS * R], start=True, stop=True)
                    mm.then_inc(s_up_q, 1)
                    mm_read = [(s_rot, j + 1), (s_q_plain, b)]
                if stage == "up_kv":
                    wait_for(kv_read)
                    pe.wait_ge(s_ckvT, [g for g, ts in enumerate(GROUPS) if j in ts][0] + 1)
                    for par in range(2):
                        mm = nc.tensor.matmul(kv_ps[:, par * 2 * D:(par + 1) * 2 * D], ckvT[:, j, par, :],
                                              w_kv[:, 0:2 * D], start=True, stop=True)
                    mm.then_inc(s_up_kv, 1)
                    kv_read = [(s_k, j + 1), (s_v, j + 1)]
                if stage == "mix_turn":
                    wait_for(turn_read)
                    pe.wait_ge(s_on, j + 1)
                    nc.tensor.transpose(turn_ps[:, 0:D], on[:, j, :], ident[:, :]).then_inc(s_onT_ps, 1)
                    turn_read = [(s_onT, j + 1)]
                if stage == "attn_out":
                    wait_for(kv_read)
                    nc.tensor.matmul(kv_ps[:, 0:D], ident[:, :], h1[:, j, :], start=True, stop=False)
                    pe.wait_ge(s_onT, j + 1)
                    nc.tensor.matmul(kv_ps[:, 0:D], onT[:, j, :], w_a[:, WOUT:WOUT + D], start=False, stop=True) \
                        .then_inc(s_h2_ps, 1)
                    kv_read = [(s_xg, j + 1), (s_h2h, j + 1)]
                if stage == "gru_in_turn":
                    wait_for(turn_read)
                    pe.wait_ge(s_xg, j + 1)
                    nc.tensor.transpose(turn_ps[:, 0:D], xg[:, j, :], ident[:, :]).then_inc(s_xgT_ps, 1)
                    turn_read = [(s_xgT, j + 1)]
                if stage == "gru_x":
                    if j == 0:
                        pe.wait_ge(s_wg, 16)
                    pe.wait_ge(s_xgT, j + 1)
                if stage in ("gru_x", "gru_x_update", "gru_x_candidate"):
                    both = xgT[:, 2 * j:2 * j + 2, :].rearrange("p s b -> p (s b)")
                if stage == "gru_x":
                    for m in range(KC):
                        if j:
                            pe.wait_ge(s_tr[m], 2 * j - 1)
                        nc.tensor.matmul(r_ps[m][:, 0:2 * B], w_x(RG, m), both, start=True, stop=False,
                                         skip_group_check=True)
                if stage == "gru_x_update":
                    for m in range(KC):
                        if j:
                            pe.wait_ge(s_tz[m], 2 * j)
                        mm = nc.tensor.matmul(z_ps[:, 2 * m * B:(2 * m + 2) * B], w_x(ZG, m), both, start=(m == 0),
                                              stop=(j == 0), skip_group_check=True)
                    if j == 0:
                        mm.then_inc(s_z_ps, 1)
                if stage == "gru_x_candidate":
                    for m in range(KC):
                        if j:
                            pe.wait_ge(s_tc[m], 2 * j)
                        mm = nc.tensor.matmul(c_ps[m][:, 0:2 * B], w_x(CG, m), both, start=True, stop=(j == 0),
                                              skip_group_check=True)
                        if j == 0:
                            mm.then_inc(s_c_ps[m], 1)
                t = j
                if stage == "gru_reset" and t:
                    if t == 1:
                        pe.wait_ge(s_scaled, 1)
                    for kc in range(KC):
                        pe.wait_ge(s_hs[kc], t)
                        for m in range(KC):
                            mm = nc.tensor.matmul(r_cols(m, t), w_h(RG, kc, m), hs[:, kc, t - 1, :], start=False,
                                                  stop=(kc == KC - 1), skip_group_check=True)
                            if kc == KC - 1:
                                mm.then_inc(s_r_ps[m], 1)
                if stage == "gru_update":
                    for m in range(KC) if t else ():
                        for kc in range(KC):
                            mm = nc.tensor.matmul(z_cols(m, t), w_h(ZG, kc, m), hs[:, kc, t - 1, :],
                                                  start=False, stop=(kc == KC - 1), skip_group_check=True)
                    if t:
                        mm.then_inc(s_z_ps, 1)
                if stage == "gru_candidate" and t:
                    if t == 1:
                        pe.wait_ge(s_scaled, 2)
                    for kc in range(KC):
                        pe.wait_ge(s_rh[kc], t)
                        for m in range(KC):
                            mm = nc.tensor.matmul(c_cols(m, t), w_h(CG, kc, m), rh[:, kc, :], start=False,
                                                  stop=(kc == KC - 1), skip_group_check=True)
                            if kc == KC - 1:
                                mm.then_inc(s_c_ps[m], 1)
                if stage == "gru_candidate" and t < T - 1:
                    if t:
                        pe.wait_ge(s_tr[0], t)
                    for _ in range(FILL[t]):
                        nc.tensor.matmul(r_ps[0][:, 2 * B:6 * B], zeros[:, 0:128], zeros[:, 0:4 * B],
                                         start=False, stop=False, skip_group_check=True)
                if stage == "out":
                    wait_for(mm_read)
                    nc.tensor.matmul(mm_ps[:, 0:D], ones[:, :], row_b[:, D:2 * D], start=True, stop=False)
                    if j == 0:
                        pe.wait_ge(s_scaled, 3)
                    for kc in range(KC):
                        pe.wait_ge(s_hs[kc], 2 * j + 2)
                        both = hs[:, kc, 2 * j:2 * j + 2, :].rearrange("p s b -> p (s b)")
                        mm = nc.tensor.matmul(mm_ps[:, 0:D], both, w_o(kc), start=False, stop=(kc == KC - 1))
                    mm.then_inc(s_out_ps, 1)
                    mm_read = [(s_ot, j + 1)]


def kernel(**inputs):
    import concourse.bacc as bacc
    from concourse.bass_utils import run_bass_kernel_spmd

    a = {n: np.asarray(w) for n, w in inputs.items()}

    def chunks(w):
        return w.reshape(-1, 128, w.shape[1]).transpose(1, 0, 2).reshape(128, -1)

    f, g = "L0_attn_", "L0_ffn_"
    pack_a = np.concatenate([chunks(a["L0_tok_W"]), a[f + "W_dq"], a[f + "W_dkv"], a[f + "W_kr"], a[f + "W_o"].T], 1)
    pack_q = np.concatenate([a[f + "W_uq"], a[f + "W_qr"], a[f + "q_ln_g"][:, None],
                             a[f + "q_ln_b"][:, None]], 1)
    pack_kv = np.concatenate([a[f + "W_ukv"], a[f + "kv_ln_g"][:, None], a[f + "kv_ln_b"][:, None]], 1)
    rows = np.stack([np.concatenate([a["L0_tok_b"], a[g + "bo"]]),
                     np.concatenate([a["L0_tok_gamma"], a["L0_tok_beta"]])])
    pack_g = np.concatenate([a[g + n].T for n in ("Wur", "Wuz", "Wu")] +
                            [chunks(a[g + n].T) for n in ("Wwr", "Wwz", "Ww", "Wo")] +
                            [chunks(a[g + n][:, None]) for n in ("bur", "buz", "bu", "bwr", "bwz", "bw")], 1)
    time = np.arange(T, dtype=np.float32)
    cos = np.repeat(np.cos(time)[:, None], HEADS * R, 1)
    sin = np.sin(time)[:, None] * np.tile(np.array([-1, 1], np.float32), HEADS)
    rot = np.stack([cos, sin], 1).reshape(NT, 2, 2, HEADS * R).astype(np.float32)
    query = np.repeat(rot.transpose(1, 0, 2, 3), B, 0)[:, :, :, None]
    keys = np.broadcast_to(rot.transpose(0, 2, 1, 3)[None], (128, NT, 2, 2, HEADS * R))
    rope = np.concatenate([query, keys], 3).reshape(128, NT, 2, ROT)
    arrays = {"x": a["x"].reshape(B, -1), "pack_a": pack_a, "pack_q": pack_q, "pack_kv": pack_kv, "rows": rows,
              "pack_g": pack_g, "rope": rope}
    arrays = {n: np.ascontiguousarray(w) for n, w in arrays.items()}
    nc = bacc.Bacc("TRN2", target_bir_lowering=False, num_devices=1)
    args = [nc.dram_tensor(n, w.shape, mybir.dt.from_np(w.dtype), kind="ExternalInput").ap() for n, w in arrays.items()]
    out = nc.dram_tensor("out", (B, T, D), F32, kind="ExternalOutput").ap()
    audio_tower(nc, *args, out)
    r = run_bass_kernel_spmd(nc, [arrays], core_ids=[0])
    return r.results[0]["out"]
```

```python
from contextlib import ExitStack

import numpy as np

import concourse.bass as bass
from concourse import mybir

F32 = mybir.dt.float32
BF16 = mybir.dt.bfloat16
ALU = mybir.AluOpType
ACT = mybir.ActivationFunctionType
AX_X = mybir.AxisListType.X

B = 64
T = 10
NT = T // 2
D = 128
PATCH = 256
HEADS, DH, R = 8, 16, 2
HD = DH + R
DQ, DKV = D // 2, 2 * D // 3
H = 256
KC = H // 128
SCALE = float(HD) ** -0.5
LOWEST = float(np.finfo(np.float32).min)
EPS_TOK, EPS = 1e-3, 1e-5

TOKW = 0
WDOWN = TOKW + 2 * D
WKR = WDOWN + DQ + DKV
WOUT = WKR + HEADS * R
PACK_A = WOUT + D
WX = 0
WH = WX + 3 * H
WO = WH + 3 * KC * H
BIAS_X = WO + KC * D
BIAS_H = BIAS_X + 3 * KC
PACK_G = BIAS_H + 3 * KC
RG, ZG, CG = range(3)
UPQ = D + HEADS * R + 2 * HEADS * R
ROT = UPQ - D
LATENT = DQ + DKV

GROUPS = [[0], [1, 2], [3, 4]]
GROUP_STAGES = ("proj", "stats_tok", "norm_tok", "stats_pre", "norm_pre", "x_norm_turn", "down", "stats_down",
                "norm_down", "down_turn", "up_q")
LAST = len(GROUPS) - 1
PART = 3
POOL_PARTS = (0, 1, 1, 2, 2)


def parts(j):
    S = 2 * j + 2
    n = -(-S // PART)
    return [(S * i // n, S * (i + 1) // n) for i in range(n)]


ORDER = [
    ("x_turn", 0), ("proj", 0), ("stats_tok", 0), ("norm_tok", 0), ("x_turn", 1), ("stats_pre", 0), ("proj", 1),
    ("norm_pre", 0), ("x_norm_turn", 0), ("down", 0), ("stats_tok", 1), ("stats_down", 0), ("norm_down", 0),
    ("scale_weights", 0), ("norm_tok", 1), ("stats_pre", 1), ("gate_bias", 0), ("down_turn", 0), ("up_q", 0),
    ("up_kv", 0), ("proj", 2), ("norm_pre", 1), ("x_norm_turn", 1), ("prod", 0, 0), ("stats_tok", 2),
    ("reduce", 0, 0), ("down", 1), ("softmax", 0), ("stats_down", 1), ("weigh", 0), ("mix", 0, 0), ("mix", 0, 1),
    ("norm_tok", 2), ("mix_norm", 0), ("mix_turn", 0), ("attn_out", 0), ("norm_down", 1), ("stats_gru", 0),
    ("down_turn", 1), ("norm_gru", 0), ("stats_pre", 2), ("up_q", 1), ("up_kv", 1), ("prod", 1, 0),
    ("gru_in_turn", 0), ("prod", 1, 1), ("gru_x", 0), ("gru_x_update", 0), ("reduce", 1, 1), ("reduce", 1, 0),
    ("scale_weights", 1), ("gru_reset", 0), ("softmax", 1), ("norm_pre", 2), ("weigh", 1), ("up_kv", 2),
    ("x_norm_turn", 2), ("mix", 1, 0), ("mix", 1, 1), ("gru_update", 0), ("mix_norm", 1), ("gru_x_candidate", 0),
    ("gru_candidate", 0), ("scale_weights", 2), ("prod", 2, 0), ("mix_turn", 1), ("attn_out", 1), ("stats_gru", 1),
    ("prod", 2, 1), ("norm_gru", 1), ("reduce", 2, 1), ("reduce", 2, 0), ("gru_reset", 1), ("gru_update", 1),
    ("down", 2), ("gru_in_turn", 1), ("stats_down", 2), ("gru_candidate", 1), ("gru_x", 1), ("gru_x_candidate", 1),
    ("softmax", 2), ("norm_down", 2), ("gru_x_update", 1), ("gru_reset", 2), ("gru_update", 2), ("down_turn", 2),
    ("weigh", 2), ("up_q", 2), ("mix", 2, 0), ("up_kv", 3), ("mix", 2, 1), ("mix_norm", 2), ("prod", 3, 0),
    ("prod", 3, 1), ("prod", 3, 2), ("gru_candidate", 2), ("reduce", 3, 2), ("mix_turn", 2), ("reduce", 3, 0),
    ("up_kv", 4), ("reduce", 3, 1), ("out", 0), ("prod", 4, 0), ("gru_reset", 3), ("attn_out", 2),
    ("stats_gru", 2), ("softmax", 3), ("prod", 4, 1), ("norm_gru", 2), ("weigh", 3), ("prod", 4, 2),
    ("reduce", 4, 2), ("gru_update", 3), ("gru_candidate", 3), ("prod", 4, 3), ("gru_in_turn", 2),
    ("reduce", 4, 3), ("gru_x", 2), ("mix", 3, 0), ("gru_reset", 4), ("gru_x_update", 2), ("mix", 3, 1),
    ("gru_x_candidate", 2), ("mix_norm", 3), ("reduce", 4, 0), ("gru_update", 4), ("gru_candidate", 4),
    ("mix_turn", 3), ("attn_out", 3), ("stats_gru", 3), ("reduce", 4, 1), ("gru_reset", 5), ("norm_gru", 3),
    ("softmax", 4), ("gru_update", 5), ("weigh", 4), ("gru_candidate", 5), ("gru_in_turn", 3), ("out", 1),
    ("gru_x", 3), ("mix", 4, 0), ("gru_x_candidate", 3), ("gru_reset", 6), ("mix", 4, 1), ("gru_x_update", 3),
    ("mix_norm", 4), ("gru_update", 6), ("gru_candidate", 6), ("mix_turn", 4), ("attn_out", 4), ("stats_gru", 4),
    ("gru_reset", 7), ("norm_gru", 4), ("gru_update", 7), ("gru_candidate", 7), ("gru_in_turn", 4), ("out", 2),
    ("gru_x", 4), ("gru_x_candidate", 4), ("gru_reset", 8), ("gru_x_update", 4), ("gru_update", 8),
    ("gru_candidate", 8), ("out", 3), ("gru_reset", 9), ("gru_update", 9), ("gru_candidate", 9), ("out_first", 4),
    ("out", 4),
]
KEEP = (2, {
    ("x_turn", 0): 3, ("proj", 0): 2, ("norm_tok", 0): 1, ("x_turn", 1): 1, ("norm_pre", 0): 2,
    ("x_norm_turn", 0): 1, ("stats_tok", 1): 2, ("norm_down", 0): 3, ("stats_pre", 1): 1, ("gate_bias", 0): 1,
    ("up_q", 0): 2, ("stats_tok", 2): 1, ("down", 1): 2, ("softmax", 0): 2, ("stats_down", 1): 1, ("weigh", 0): 1,
    ("norm_tok", 2): 1, ("mix_norm", 0): 5, ("mix_turn", 0): 2, ("attn_out", 0): 4, ("gru_in_turn", 0): 3,
})
FILL = (7, 1, 0, 5, 0, 2, 0, 0, 0)


def audio_tower(nc, x, pack_a, pack_q, pack_kv, rows, pack_g, rope, out):
    with ExitStack() as ctx:
        def sb(name, shape, dt=F32):
            return ctx.enter_context(nc.sbuf_tensor(name, shape, dt))

        def bank(name):
            return ctx.enter_context(nc.psum_tensor(name, [128, 512], F32))

        def sem(name):
            return ctx.enter_context(nc.semaphore(name))

        w_a = sb("w_a", [128, PACK_A])
        w_q = sb("w_q", [DQ, D + HEADS * R + 2])
        w_kv = sb("w_kv", [DKV, 2 * D + 2])
        w_g = sb("w_g", [128, PACK_G])
        w_hs = sb("w_hs", [128, 3 * KC * H + KC * D])
        half_bias = sb("half_bias", [128, 3 * KC])
        row_b = sb("row_b", [1, 2 * D])
        gamma_b = sb("gamma_b", [128, 2 * D])
        cs = sb("cs", [128, NT, 2, ROT])
        ident = sb("ident", [128, 128])
        ones = sb("ones", [1, 128])
        minus_half = sb("minus_half", [128, 8])
        zeros = sb("zeros", [128, 512], BF16)
        warm = sb("warm", [128, 1])
        x_sb = sb("x_sb", [B, (T + 1) * D])
        xT = sb("xT", [128, (T + 1) * B])
        hn = sb("hn", [128, NT, D])
        hg = sb("hg", [128, NT, D])
        h1 = sb("h1", [128, NT, D])
        xn = sb("xn", [128, NT, D])
        xnT = sb("xnT", [128, NT, D])
        xnT2 = sb("xnT2", [128, NT, 2, 2 * B])
        ckvT = sb("ckvT", [DKV, NT, 2, 2 * B])
        cn = sb("cn", [128, NT, LATENT])
        cqT = sb("cqT", [DQ, NT, D])
        q = sb("q", [128, NT, HEADS, HD])
        k = sb("k", [128, T, HEADS, HD])
        v = sb("v", [128, T, HEADS, DH])
        rot = sb("rot", [128, NT, ROT])
        rot_cos = sb("rot_cos", [128, NT, ROT])
        rot_sin = sb("rot_sin", [128, NT, ROT])
        prod = sb("prod", [128, T, HEADS, HD])
        sc = sb("sc", [128, T, HEADS])
        scm = sb("scm", [128, T, HEADS])
        p = sb("p", [128, T, HEADS])
        mx = sb("mx", [128, HEADS])
        den = sb("den", [128, HEADS])
        rden = sb("rden", [128, HEADS])
        prod_v = sb("prod_v", [128, T, HEADS, DH])
        mixed = sb("mixed", [128, D])
        on = sb("on", [128, NT, D])
        onT = sb("onT", [128, NT, D])
        h2h = sb("h2h", [128, NT, D])
        xg = sb("xg", [128, NT, D])
        xgT = sb("xgT", [128, T, B])
        stats = sb("stats", [128, NT, 5, 6])
        mv = sb("mv", [128, NT, 5, 2])
        ve = sb("ve", [128, 5, NT])
        rstd = sb("rstd", [128, 5, NT])
        shift = sb("shift", [128, 5, NT])
        hs = sb("hs", [128, KC, T, B])
        tr = sb("tr", [128, KC, B])
        tz = sb("tz", [128, KC, B])
        tc = sb("tc", [128, KC, B])
        rh = sb("rh", [128, KC, B])
        keep = sb("keep", [128, KC, B])
        move = sb("move", [128, KC, B])
        ot = sb("ot", [128, NT, D])
        o = sb("o", [128, NT, D])

        turn_ps = bank("turn_ps")
        mm_ps = bank("mm_ps")
        kv_ps = bank("kv_ps")
        r_ps = [bank(f"r_ps{m}") for m in range(KC)]
        z_ps = bank("z_ps")
        c_ps = [bank(f"c_ps{m}") for m in range(KC)]

        s_x_first = sem("s_x_first")
        s_x = sem("s_x")
        s_w_tok = sem("s_w_tok")
        s_wa = sem("s_wa")
        s_wq = sem("s_wq")
        s_wkv = sem("s_wkv")
        s_rows = sem("s_rows")
        s_gamma = sem("s_gamma")
        s_rope = sem("s_rope")
        s_wg = sem("s_wg")
        s_const = sem("s_const")
        s_zeros = sem("s_zeros")
        s_warm = sem("s_warm")
        s_ident = sem("s_ident")
        s_scaled = sem("s_scaled")
        s_hbias = sem("s_hbias")
        s_xT_ps = sem("s_xT_ps")
        s_xT = sem("s_xT")
        s_proj = sem("s_proj")
        NORMS = ("tok", "pre", "down", "gru")
        s_stats = {n: sem(f"s_stats_{n}") for n in NORMS}
        s_mv = {n: sem(f"s_mv_{n}") for n in NORMS}
        s_ve = {n: sem(f"s_ve_{n}") for n in NORMS}
        s_rstd = {n: sem(f"s_rstd_{n}") for n in NORMS}
        s_shift = {n: sem(f"s_shift_{n}") for n in NORMS}
        s_hn = sem("s_hn")
        s_hn_act = sem("s_hn_act")
        s_hg = sem("s_hg")
        s_h1 = sem("s_h1")
        s_xn = sem("s_xn")
        s_xn_act = sem("s_xn_act")
        s_xnT_ps = sem("s_xnT_ps")
        s_xnT = sem("s_xnT")
        s_xnT2 = sem("s_xnT2")
        s_down = sem("s_down")
        s_cn = sem("s_cn")
        s_cn_act = sem("s_cn_act")
        s_cT_ps = sem("s_cT_ps")
        s_cqT = sem("s_cqT")
        s_ckvT = sem("s_ckvT")
        s_up_q = sem("s_up_q")
        s_up_kv = sem("s_up_kv")
        s_rot = sem("s_rot")
        s_q_plain = sem("s_q_plain")
        s_rot_parts = sem("s_rot_parts")
        s_q_rot = sem("s_q_rot")
        s_k_rot = sem("s_k_rot")
        s_k = sem("s_k")
        s_v = sem("s_v")
        s_prod = sem("s_prod")
        s_prod_pool = sem("s_prod_pool")
        s_sc = sem("s_sc")
        s_masked = sem("s_masked")
        s_mx = sem("s_mx")
        s_scm = sem("s_scm")
        s_p = sem("s_p")
        s_den = sem("s_den")
        s_rden = sem("s_rden")
        s_prod_v = sem("s_prod_v")
        s_mixed = sem("s_mixed")
        s_on = sem("s_on")
        s_onT_ps = sem("s_onT_ps")
        s_onT = sem("s_onT")
        s_h2_ps = sem("s_h2_ps")
        s_h2h = sem("s_h2h")
        s_xg = sem("s_xg")
        s_xgT_ps = sem("s_xgT_ps")
        s_xgT = sem("s_xgT")
        s_r_ps = [sem(f"s_r_ps{m}") for m in range(KC)]
        s_z_ps = sem("s_z_ps")
        s_c_ps = [sem(f"s_c_ps{m}") for m in range(KC)]
        s_tr = [sem(f"s_tr{m}") for m in range(KC)]
        s_tz = [sem(f"s_tz{m}") for m in range(KC)]
        s_tc = [sem(f"s_tc{m}") for m in range(KC)]
        s_rh = [sem(f"s_rh{m}") for m in range(KC)]
        s_keep = sem("s_keep")
        s_move = [sem(f"s_move{m}") for m in range(KC)]
        s_hs = [sem(f"s_hs{m}") for m in range(KC)]
        s_out_ps = sem("s_out_ps")
        s_ot = sem("s_ot")
        s_o = sem("s_o")
        s_stored = sem("s_stored")

        block = ctx.enter_context(nc.Block())

        def w_x(g, m):
            return w_g[:, WX + g * H + m * 128:WX + g * H + (m + 1) * 128]

        def w_h(g, kc, m):
            at = (g * KC + kc) * H + m * 128
            return w_hs[:, at:at + 128]

        def w_o(kc):
            at = 3 * KC * H + kc * D
            return w_hs[:, at:at + D]

        def r_cols(m, t):
            return r_ps[m][:, (t % 2) * B:(t % 2 + 1) * B]

        def z_cols(m, t):
            return z_ps[:, (2 * m + t % 2) * B:(2 * m + t % 2 + 1) * B]

        def c_cols(m, t):
            return c_ps[m][:, (t % 2) * B:(t % 2 + 1) * B]

        def parts_done(j):
            return sum(len(parts(i)) for i in range(j))

        def tiles_done(g):
            return GROUPS[g][-1] + 1

        def affine_tok(eng, nc_eng, g):
            a, b = GROUPS[g][0], tiles_done(g)
            gains = gamma_b[:, 0:D].unsqueeze(1).broadcast_to([128, b - a, D])
            shifts = gamma_b[:, D:2 * D].unsqueeze(1).broadcast_to([128, b - a, D])
            eng.wait_ge(*((s_hn, b) if g < LAST else (s_hn_act, b - a)))
            eng.wait_ge(s_gamma, 16)
            nc_eng.tensor_tensor(hg[:, a:b, :], hn[:, a:b, :], gains, ALU.mult).then_inc(s_hg, 1)
            eng.wait_ge(s_hg, g + 1)
            nc_eng.tensor_tensor(h1[:, a:b, :], hg[:, a:b, :], shifts, ALU.add).then_inc(s_h1, 1)

        def rotate(eng, nc_eng, g):
            a, b = GROUPS[g][0], tiles_done(g)
            eng.wait_ge(s_rot, g + 1)
            if g == 0:
                eng.wait_ge(s_rope, 16)
            else:
                eng.wait_ge(s_k_rot, a)
            nc_eng.tensor_tensor(rot_cos[:, a:b, :], rot[:, a:b, :], cs[:, a:b, 0, :], ALU.mult) \
                .then_inc(s_rot_parts, 1)
            sins = cs[:, a:b, 1, :].rearrange("p j (h r) -> p j h r", r=R)
            rots = rot[:, a:b, :].rearrange("p j (h r) -> p j h r", r=R)
            dst = rot_sin[:, a:b, :].rearrange("p j (h r) -> p j h r", r=R)
            for r in range(R):
                nc_eng.tensor_tensor(dst[:, :, :, r], rots[:, :, :, 1 - r], sins[:, :, :, r], ALU.mult) \
                    .then_inc(s_rot_parts, 1)
            eng.wait_ge(s_rot_parts, 3 * (g + 1))
            qr = HEADS * R
            for i in range(a, b):
                cos_i, sin_i = rot_cos[:, i, :], rot_sin[:, i, :]
                nc_eng.tensor_tensor(q[:, i, :, DH:HD], cos_i[:, 0:qr].rearrange("p (h r) -> p h r", r=R),
                                     sin_i[:, 0:qr].rearrange("p (h r) -> p h r", r=R), ALU.add) \
                    .then_inc(s_q_rot, 1)
                nc_eng.tensor_tensor(k[:, 2 * i:2 * i + 2, :, DH:HD],
                                     cos_i[:, qr:].rearrange("p (s h r) -> p s h r", s=2, r=R),
                                     sin_i[:, qr:].rearrange("p (s h r) -> p s h r", s=2, r=R), ALU.add) \
                    .then_inc(s_k_rot, 1)

        def query_key_products(eng, nc_eng, j, i):
            lo, hi = parts(j)[i]
            eng.wait_ge(s_q_rot, j + 1)
            eng.wait_ge(s_q_plain, j + 1)
            eng.wait_ge(s_k_rot, j + 1)
            eng.wait_ge(s_k, j + 1)
            flat = "p s h d -> p s (h d)"
            queries = q[:, j:j + 1, :, :].rearrange(flat).broadcast_to([128, hi - lo, HEADS * HD])
            return nc_eng.tensor_tensor(prod[:, lo:hi, :, :].rearrange(flat), k[:, lo:hi, :, :].rearrange(flat),
                                        queries, ALU.mult)

        def weighted_values(eng, nc_eng, j):
            S = 2 * j + 2
            eng.wait_ge(s_p, j + 1)
            eng.wait_ge(s_v, j + 1)
            if j:
                eng.wait_ge(s_mixed, 2 * j)
            weights = p[:, 0:S, :].rearrange("p s h -> p (s h)").unsqueeze(2).broadcast_to([128, S * HEADS, DH])
            nc_eng.tensor_tensor(prod_v[:, 0:S, :, :].rearrange("p s h d -> p (s h) d"),
                                 v[:, 0:S, :, :].rearrange("p s h d -> p (s h) d"), weights, ALU.mult) \
                .then_inc(s_prod_v, 1)

        @block.sync
        def _(sp):
            sp.dma_start(x_sb[:, 0:3 * D], x[:, 0:3 * D]).then_inc(s_x_first, 16)
            sp.dma_start(x_sb[:, 3 * D:], x[:, 3 * D:(T + 1) * D]).then_inc(s_x, 16)
            sp.dma_start(gamma_b[:, :], rows[1:2, :].broadcast_to([128, 2 * D])).then_inc(s_gamma, 16)
            sp.dma_start(w_a[:, WDOWN:], pack_a[:, WDOWN:]).then_inc(s_wa, 16)
            sp.dma_start(w_q[:, :], pack_q).then_inc(s_wq, 16)
            sp.dma_start(w_kv[:, :], pack_kv).then_inc(s_wkv, 16)
            sp.dma_start(cs[:, :, :, :], rope).then_inc(s_rope, 16)
            sp.dma_start(w_g[:, :], pack_g).then_inc(s_wg, 16)
            for stage, j, *_ in ORDER:
                if stage == "out_first":
                    sp.wait_ge(s_o, NT)
                    sp.dma_start(out[:, 2 * j, :], o[0:B, j, :]).then_inc(s_stored, 16)
                if stage == "out":
                    sp.wait_ge(s_o, j + 1 + (j == NT - 1))
                    for par in range(j == NT - 1, 2):
                        sp.dma_start(out[:, 2 * j + par, :], o[par * B:(par + 1) * B, j, :]).then_inc(s_stored, 16)
            sp.wait_ge(s_stored, 16 * T)

        @block.gpsimd
        def _(pool):
            nc.gpsimd.memset(warm[:, :], 0.0).then_inc(s_warm, 1)
            nc.gpsimd.memset(ident[:, :], 0.0).then_inc(s_const, 1)
            nc.gpsimd.memset(ones[:, :], 1.0).then_inc(s_const, 1)
            nc.gpsimd.memset(minus_half[:, :], -0.5).then_inc(s_const, 1)
            pool.wait_ge(s_const, 3)
            nc.gpsimd.affine_select(out=ident[:, :], in_=ident[:, :], compare_op=ALU.not_equal, fill=1.0, base=0,
                                    pattern=[[-1, 128]], channel_multiplier=1).then_inc(s_ident, 1)

            def group_power(name, at, n, g, eps):
                a, b = GROUPS[g][0], GROUPS[g][-1] + 1
                pool.wait_ge(s_mv[name], n * b)
                nc.gpsimd.tensor_scalar(ve[:, at:at + n, a:b], mv[:, a:b, at:at + n, 1].rearrange("p j n -> p n j"),
                                        1.0, eps, ALU.mult, ALU.add).then_inc(s_ve[name], 1)
                pool.wait_ge(s_ve[name], g + 1)
                half = minus_half[:, 0:n * (b - a)].rearrange("p (n j) -> p n j", n=n)
                nc.gpsimd.tensor_tensor(rstd[:, at:at + n, a:b], ve[:, at:at + n, a:b], half,
                                        ALU.pow).then_inc(s_rstd[name], 1)

            for stage, j, *part in ORDER:
                a, b = (GROUPS[j][0], GROUPS[j][-1] + 1) if stage in GROUP_STAGES else (j, j + 1)
                if stage == "stats_tok":
                    group_power("tok", 0, 1, j, EPS_TOK)
                if stage == "stats_pre":
                    group_power("pre", 1, 1, j, EPS)
                if stage == "stats_down":
                    group_power("down", 2, 2, j, EPS)
                if stage == "norm_tok" and j == len(GROUPS) - 1:
                    affine_tok(pool, nc.gpsimd, j)
                if stage == "scale_weights":
                    lo, hi, factor = ((0, 2 * KC * H, 0.5), (2 * KC * H, 3 * KC * H, 0.25),
                                      (3 * KC * H, 3 * KC * H + KC * D, 0.5))[j]
                    pool.wait_ge(s_wg, 16)
                    nc.gpsimd.tensor_scalar(w_hs[:, lo:hi], w_g[:, WH + lo:WH + hi], factor, 1.0, ALU.mult,
                                            ALU.mult).then_inc(s_scaled, 1)
                if stage == "up_q":
                    if j == len(GROUPS) - 1:
                        rotate(pool, nc.gpsimd, j)
                if stage == "prod" and part[0] < POOL_PARTS[j]:
                    pool.wait_ge(s_sc, parts_done(j))
                    query_key_products(pool, nc.gpsimd, j, part[0]).then_inc(s_prod_pool, 1)
                if stage == "weigh" and j:
                    weighted_values(pool, nc.gpsimd, j)
                if stage == "stats_gru":
                    pool.wait_ge(s_mv["gru"], j + 1)
                    nc.gpsimd.tensor_scalar(ve[:, 4, j:j + 1], mv[:, j, 4, 1:2], 1.0, EPS, ALU.mult, ALU.add) \
                        .then_inc(s_ve["gru"], 1)
                    pool.wait_ge(s_ve["gru"], j + 1)
                    nc.gpsimd.tensor_tensor(rstd[:, 4, j:j + 1], ve[:, 4, j:j + 1], minus_half[:, 0:1], ALU.pow) \
                        .then_inc(s_rstd["gru"], 1)

        @block.scalar
        def _(act):
            act.dma_start(w_a[:, 0:WDOWN], pack_a[:, 0:WDOWN]).then_inc(s_w_tok, 16)
            act.wait_ge(s_warm, 1)
            nc.scalar.activation(warm[:, :], warm[:, :], ACT.Tanh)
            act.dma_start(row_b[:, :], rows[0:1, :]).then_inc(s_rows, 16)

            def shifted(dst, src, j, at):
                return nc.scalar.activation(dst, src, ACT.Identity, bias=shift[:, at, j:j + 1],
                                            scale=rstd[:, at, j:j + 1])

            for stage, j, *_ in ORDER:
                a, b = (GROUPS[j][0], GROUPS[j][-1] + 1) if stage in GROUP_STAGES else (j, j + 1)
                n = b - a
                if stage == "norm_tok" and j == LAST:
                    act.wait_ge(s_shift["tok"], 1)
                    for i in range(n):
                        shifted(hn[:, a + i, :], mm_ps[:, i * D:(i + 1) * D], a + i, 0).then_inc(s_hn_act, 1)
                if stage == "norm_pre" and j:
                    act.wait_ge(s_shift["pre"], j)
                    shifted(xn[:, b - 1, :], h1[:, b - 1, :], b - 1, 1).then_inc(s_xn_act, 1)
                if stage == "norm_down" and j == LAST:
                    act.wait_ge(s_shift["down"], 1)
                    for i in range(n):
                        for s, c, d in ((2, 0, DQ), (3, DQ, LATENT)):
                            shifted(cn[:, a + i, c:d], kv_ps[:, i * LATENT + c:i * LATENT + d], a + i, s) \
                                .then_inc(s_cn_act, 1)
                if stage == "norm_gru" and j:
                    act.wait_ge(s_shift["gru"], j)
                    shifted(xg[:, j, :], kv_ps[:, 0:D], j, 4).then_inc(s_xg, 1)
                if stage == "x_turn":
                    act.wait_ge(s_xT_ps, j + 1)
                    if j == 0:
                        nc.scalar.copy(xT[:, 0:3 * B], turn_ps[:, 0:3 * B]).then_inc(s_xT, 1)
                    else:
                        nc.scalar.copy(xT[:, 3 * B:], kv_ps[:, 0:(T - 2) * B]).then_inc(s_xT, 1)
                if stage == "x_norm_turn":
                    act.wait_ge(s_xnT_ps, j + 1)
                    nc.scalar.copy(xnT[:, a:b, :].rearrange("p j c -> p (j c)"), turn_ps[:, 0:n * D]).then_inc(s_xnT, 1)
                    nc.scalar.copy(xnT2[:, a:b, :, :].rearrange("p j s (e b) -> p (j s) e b", e=2),
                                   turn_ps[:, 0:n * D].rearrange("p (s b) -> p s b", b=B).unsqueeze(2)
                                   .broadcast_to([128, 2 * n, 2, B])).then_inc(s_xnT2, 1)
                if stage == "down_turn":
                    act.wait_ge(s_cT_ps, j + 1)
                    if j == 0:
                        act.wait_ge(s_wq, 16)
                        act.wait_ge(s_wkv, 16)
                    nc.scalar.activation(cqT[:, a:b, :].rearrange("p j c -> p (j c)"), turn_ps[0:DQ, 0:n * D],
                                         ACT.Identity, bias=w_q[:, D + HEADS * R + 1:D + HEADS * R + 2],
                                         scale=w_q[:, D + HEADS * R:D + HEADS * R + 1]).then_inc(s_cqT, 1)
                    nc.scalar.activation(ckvT[:, a:b, :, :].rearrange("p j s (e b) -> p (j s) e b", e=2),
                                         turn_ps[0:DKV, n * D:2 * n * D].rearrange("p (s b) -> p s b", b=B)
                                         .unsqueeze(2).broadcast_to([DKV, 2 * n, 2, B]), ACT.Identity,
                                         bias=w_kv[:, 2 * D + 1:2 * D + 2], scale=w_kv[:, 2 * D:2 * D + 1]) \
                        .then_inc(s_ckvT, 1)
                if stage == "up_q":
                    act.wait_ge(s_up_q, j + 1)
                    up = mm_ps[:, 0:n * UPQ].rearrange("p (j c) -> p j c", j=n)
                    nc.scalar.copy(rot[:, a:b, :], up[:, :, D:UPQ]).then_inc(s_rot, 1)
                    for i in range(n):
                        nc.scalar.copy(q[:, a + i, :, 0:DH], up[:, i, 0:D].rearrange("p (h d) -> p h d", h=HEADS)) \
                            .then_inc(s_q_plain, 1)
                if stage == "up_kv":
                    act.wait_ge(s_up_kv, j + 1)
                    kv = kv_ps[:, :].rearrange("p (s e h d) -> p s e h d", s=2, e=2, h=HEADS)
                    nc.scalar.copy(k[:, 2 * j:2 * j + 2, :, 0:DH], kv[:, :, 0, :, :]).then_inc(s_k, 1)
                    nc.scalar.copy(v[:, 2 * j:2 * j + 2, :, :], kv[:, :, 1, :, :]).then_inc(s_v, 1)
                if stage == "softmax":
                    act.wait_ge(s_scm, j + 1)
                    if j:
                        act.wait_ge(s_prod_v, j)
                        act.wait_ge(s_den, j)
                    S = 2 * j + 2
                    nc.scalar.activation(p[:, 0:S, :], scm[:, 0:S, :], ACT.Exp, scale=SCALE).then_inc(s_p, 1)
                if stage == "mix_turn":
                    act.wait_ge(s_onT_ps, j + 1)
                    nc.scalar.copy(onT[:, j, :], turn_ps[:, 0:D]).then_inc(s_onT, 1)
                if stage == "stats_gru":
                    act.wait_ge(s_stats["gru"], j + 1)
                    nc.scalar.activation(h2h[:, j, :], kv_ps[:, 0:D], ACT.Copy, bias=0.5).then_inc(s_h2h, 1)
                if stage == "gru_in_turn":
                    act.wait_ge(s_xgT_ps, j + 1)
                    nc.scalar.copy(xgT[:, 2 * j:2 * j + 2, :],
                                   turn_ps[:, 0:D].rearrange("p (s b) -> p s b", s=2)).then_inc(s_xgT, 1)
                t = j
                if stage == "gru_reset" and t:
                    for m in range(KC):
                        act.wait_ge(s_r_ps[m], t)
                        nc.scalar.activation(tr[:, m, :], r_cols(m, t), ACT.Tanh, scale=0.5,
                                             bias=half_bias[:, m:m + 1]).then_inc(s_tr[m], 1)
                if stage == "gru_update":
                    if t == 0:
                        act.wait_ge(s_hbias, 2)
                    act.wait_ge(s_z_ps, t + 1)
                    for m in range(KC):
                        nc.scalar.activation(tz[:, m, :], z_cols(m, t), ACT.Tanh, scale=0.5,
                                             bias=half_bias[:, KC + m:KC + m + 1]).then_inc(s_tz[m], 1)
                if stage == "gru_candidate":
                    for m in range(KC):
                        act.wait_ge(s_c_ps[m], t + 1)
                        nc.scalar.activation(tc[:, m, :], c_cols(m, t), ACT.Tanh,
                                             bias=half_bias[:, 2 * KC + m:2 * KC + m + 1]).then_inc(s_tc[m], 1)
                if stage == "out_first":
                    act.wait_ge(s_out_ps, NT)
                    nc.scalar.activation(ot[0:B, j, :], mm_ps[0:B, 0:D], ACT.Tanh, scale=0.5).then_inc(s_ot, 1)
                if stage == "out":
                    act.wait_ge(s_out_ps, j + 1 + (j == NT - 1))
                    rows_ = slice(B, 2 * B) if j == NT - 1 else slice(0, 2 * B)
                    nc.scalar.activation(ot[rows_, j, :], mm_ps[rows_, 0:D], ACT.Tanh, scale=0.5).then_inc(s_ot, 1)

        @block.vector
        def _(dve):
            nc.vector.memset(zeros[:, :], 0.0).then_inc(s_zeros, 1)
            stats_done = {n: 0 for n in NORMS}

            def moments(name, rows_):
                for j, at, src in rows_:
                    nc.vector.bn_stats(stats[:, j, at, :], src).then_inc(s_stats[name], 1)
                for j, at, src in rows_:
                    stats_done[name] += 1
                    dve.wait_ge(s_stats[name], stats_done[name])
                    nc.vector.bn_aggr(mv[:, j, at, :], stats[:, j, at, :]).then_inc(s_mv[name], 1)

            def normed(dst, src, j, at):
                return nc.vector.tensor_scalar(dst, src, mv[:, j, at, 0:1], rstd[:, at, j:j + 1], ALU.subtract,
                                               ALU.mult)

            def shifts(name, a, b, at, n):
                if a:
                    nc.vector.scalar_tensor_tensor(out=shift[:, at:at + n, a:b],
                                                   in0=mv[:, a:b, at:at + n, 0].rearrange("p j n -> p n j"),
                                                   scalar=-1.0, in1=rstd[:, at:at + n, a:b], op0=ALU.mult,
                                                   op1=ALU.mult).then_inc(s_shift[name], 1)

            for stage, j, *part in ORDER:
                a, b = (GROUPS[j][0], GROUPS[j][-1] + 1) if stage in GROUP_STAGES else (j, j + 1)
                n = b - a
                if stage == "stats_tok":
                    dve.wait_ge(s_proj, j + 1)
                    moments("tok", [(a + i, 0, mm_ps[:, i * D:(i + 1) * D]) for i in range(n)])
                if stage == "norm_tok":
                    dve.wait_ge(s_rstd["tok"], j + 1)
                    if j == LAST:
                        shifts("tok", a, b, 0, 1)
                    for i in range(n) if j < LAST else ():
                        normed(hn[:, a + i, :], mm_ps[:, i * D:(i + 1) * D], a + i, 0).then_inc(s_hn, 1)
                    if j < len(GROUPS) - 1:
                        affine_tok(dve, nc.vector, j)
                if stage == "stats_pre":
                    dve.wait_ge(s_h1, j + 1)
                    moments("pre", [(i, 1, h1[:, i, :]) for i in range(a, b)])
                if stage == "norm_pre":
                    dve.wait_ge(s_rstd["pre"], j + 1)
                    shifts("pre", a, b, 1, 1)
                    normed(xn[:, a, :], h1[:, a, :], a, 1).then_inc(s_xn, 1)
                if stage == "stats_down":
                    dve.wait_ge(s_down, j + 1)
                    moments("down", [(a + i, s, kv_ps[:, i * LATENT + c:i * LATENT + d])
                                     for i in range(n) for s, c, d in ((2, 0, DQ), (3, DQ, LATENT))])
                if stage == "norm_down":
                    dve.wait_ge(s_rstd["down"], j + 1)
                    if j == LAST:
                        shifts("down", a, b, 2, 2)
                    for i in range(n) if j < LAST else ():
                        for s, c, d in ((2, 0, DQ), (3, DQ, LATENT)):
                            normed(cn[:, a + i, c:d], kv_ps[:, i * LATENT + c:i * LATENT + d], a + i, s) \
                                .then_inc(s_cn, 1)
                if stage == "up_q" and j < len(GROUPS) - 1:
                    rotate(dve, nc.vector, j)
                S = 2 * j + 2
                if stage == "prod" and part[0] >= POOL_PARTS[j]:
                    if j:
                        dve.wait_ge(s_sc, parts_done(j))
                    query_key_products(dve, nc.vector, j, part[0]).then_inc(s_prod, 1)
                if stage == "reduce":
                    lo, hi = parts(j)[part[0]]
                    if j:
                        dve.wait_ge(s_scm, j)
                    if part[0] < POOL_PARTS[j]:
                        dve.wait_ge(s_prod_pool, sum(POOL_PARTS[:j]) + part[0] + 1)
                    else:
                        dve.wait_ge(s_prod, parts_done(j) - sum(POOL_PARTS[:j + 1]) + part[0] + 1)
                    nc.vector.tensor_reduce(sc[:, lo:hi, :], prod[:, lo:hi, :, :], AX_X, ALU.add).then_inc(s_sc, 1)
                if stage == "softmax":
                    dve.wait_ge(s_sc, parts_done(j + 1))
                    nc.vector.memset(sc[0:B, S - 1, :], LOWEST).then_inc(s_masked, 1)
                    dve.wait_ge(s_masked, j + 1)
                    nc.vector.tensor_reduce(mx[:, :], sc[:, 0:S, :].rearrange("p s h -> p h s"), AX_X, ALU.max) \
                        .then_inc(s_mx, 1)
                    dve.wait_ge(s_mx, j + 1)
                    if j:
                        dve.wait_ge(s_p, j)
                    nc.vector.tensor_tensor(scm[:, 0:S, :], sc[:, 0:S, :],
                                            mx[:, :].unsqueeze(1).broadcast_to([128, S, HEADS]), ALU.subtract) \
                        .then_inc(s_scm, 1)
                if stage == "weigh":
                    if j == 0:
                        weighted_values(dve, nc.vector, j)
                    dve.wait_ge(s_p, j + 1)
                    if j:
                        dve.wait_ge(s_on, j)
                    nc.vector.tensor_reduce(den[:, :], p[:, 0:S, :].rearrange("p s h -> p h s"), AX_X, ALU.add) \
                        .then_inc(s_den, 1)
                    dve.wait_ge(s_den, j + 1)
                    nc.vector.reciprocal(rden[:, :], den[:, :]).then_inc(s_rden, 1)
                if stage == "mix":
                    dve.wait_ge(s_prod_v, j + 1)
                    half = slice(part[0] * (D // 2), (part[0] + 1) * (D // 2))
                    nc.vector.tensor_reduce(mixed[:, half],
                                            prod_v[:, 0:S, :, :].rearrange("p s h d -> p (h d) s")[:, half, :], AX_X,
                                            ALU.add).then_inc(s_mixed, 1)
                if stage == "mix_norm":
                    dve.wait_ge(s_mixed, 2 * (j + 1))
                    dve.wait_ge(s_rden, j + 1)
                    nc.vector.tensor_tensor(on[:, j, :].rearrange("p (h d) -> p h d", h=HEADS),
                                            mixed[:, :].rearrange("p (h d) -> p h d", h=HEADS),
                                            rden[:, :].unsqueeze(2).broadcast_to([128, HEADS, DH]), ALU.mult) \
                        .then_inc(s_on, 1)
                if stage == "stats_gru":
                    dve.wait_ge(s_h2_ps, j + 1)
                    moments("gru", [(j, 4, kv_ps[:, 0:D])])
                if stage == "norm_gru":
                    dve.wait_ge(s_rstd["gru"], j + 1)
                    if j == 0:
                        dve.wait_ge(s_h2h, j + 1)
                        normed(xg[:, j, :], kv_ps[:, 0:D], j, 4).then_inc(s_xg, 1)
                    shifts("gru", a, b, 4, 1)
                t = j
                if stage == "gate_bias":
                    dve.wait_ge(s_wg, 16)
                    nc.vector.tensor_tensor(half_bias[:, :], w_g[:, BIAS_X:BIAS_X + 3 * KC],
                                            w_g[:, BIAS_H:BIAS_H + 3 * KC], ALU.add).then_inc(s_hbias, 1)
                    dve.wait_ge(s_hbias, 1)
                    nc.vector.tensor_scalar(half_bias[:, 0:2 * KC], half_bias[:, 0:2 * KC], 0.5, None,
                                            ALU.mult).then_inc(s_hbias, 1)
                if stage == "gru_reset":
                    for m in range(KC) if t else ():
                        dve.wait_ge(s_tr[m], t)
                        nc.vector.scalar_tensor_tensor(out=rh[:, m, :], in0=tr[:, m, :], scalar=1.0,
                                                       in1=hs[:, m, t - 1, :], op0=ALU.add, op1=ALU.mult) \
                            .then_inc(s_rh[m], 1)
                if stage == "gru_update" and t:
                    for m in range(KC):
                        dve.wait_ge(s_tz[m], t + 1)
                    nc.vector.scalar_tensor_tensor(out=keep[:, :, :], in0=tz[:, :, :], scalar=1.0,
                                                   in1=hs[:, :, t - 1, :], op0=ALU.add, op1=ALU.mult) \
                        .then_inc(s_keep, 1)
                if stage == "gru_candidate":
                    for m in range(KC):
                        dve.wait_ge(s_tc[m], t + 1)
                        nc.vector.scalar_tensor_tensor(out=move[:, m, :], in0=tz[:, m, :], scalar=1.0,
                                                       in1=tc[:, m, :], op0=ALU.subtract, op1=ALU.mult) \
                            .then_inc(s_move[m], 1)
                        dve.wait_ge(s_move[m], t + 1)
                        if t:
                            dve.wait_ge(s_keep, t)
                            nc.vector.scalar_tensor_tensor(out=hs[:, m, t, :], in0=keep[:, m, :], scalar=0.5,
                                                           in1=move[:, m, :], op0=ALU.mult, op1=ALU.subtract) \
                                .then_inc(s_hs[m], 1)
                        else:
                            nc.vector.tensor_scalar(hs[:, m, t, :], move[:, m, :], -1.0, None, ALU.mult) \
                                .then_inc(s_hs[m], 1)
                if stage in ("out_first", "out"):
                    last = stage == "out" and j == NT - 1
                    rows_ = slice(0, B) if stage == "out_first" else slice(B if last else 0, 2 * B)
                    dve.wait_ge(s_ot, j + 1 + last)
                    nc.vector.scalar_tensor_tensor(out=o[rows_, j, :], in0=ot[rows_, j, :], scalar=0.5,
                                                   in1=h2h[rows_, j, :], op0=ALU.mult, op1=ALU.add) \
                        .then_inc(s_o, 1)

        @block.tensor
        def _(pe):
            turn_read, mm_read, kv_read = [], [], []

            def wait_for(read):
                for s, n in read:
                    pe.wait_ge(s, n)

            def keep_clock(n):
                for _ in range(n):
                    nc.tensor.matmul(c_ps[1][:, :], zeros[:, 0:128], zeros[:, :], start=True, stop=True)

            pe.wait_ge(s_zeros, 1)
            keep_clock(KEEP[0])
            pe.wait_ge(s_ident, 1)
            before_gru = True
            for stage, j, *_ in ORDER:
                a, b = (GROUPS[j][0], GROUPS[j][-1] + 1) if stage in GROUP_STAGES else (j, j + 1)
                n = b - a
                if stage == "gru_x" and j == 0:
                    before_gru = False
                if before_gru:
                    keep_clock(KEEP[1].get((stage, j), 0))
                if stage == "x_turn":
                    pe.wait_ge(*((s_x_first, 16) if j == 0 else (s_x, 16)))
                    lo, hi, dst = (0, 3, turn_ps) if j == 0 else (3, T + 1, kv_ps)
                    for c in range(lo, hi):
                        mm = nc.tensor.transpose(dst[:, (c - lo) * B:(c - lo + 1) * B], x_sb[:, c * D:(c + 1) * D],
                                                 ident[0:B, 0:B])
                    mm.then_inc(s_xT_ps, 1)
                    if j == 0:
                        turn_read = [(s_xT, 1)]
                    else:
                        kv_read = [(s_xT, 2)]
                if stage == "proj":
                    wait_for(mm_read)
                    pe.wait_ge(s_xT, min(j + 1, 2))
                    if j == 0:
                        pe.wait_ge(s_w_tok, 16)
                    for i in range(n):
                        for e in range(2):
                            at = (2 * (a + i) + e) * B
                            nc.tensor.matmul(mm_ps[:, i * D:(i + 1) * D], xT[:, at:at + 2 * B],
                                             w_a[:, TOKW + e * D:TOKW + (e + 1) * D], start=(e == 0), stop=False)
                        if j == 0:
                            pe.wait_ge(s_rows, 16)
                            pe.wait_ge(s_const, 3)
                        mm = nc.tensor.matmul(mm_ps[:, i * D:(i + 1) * D], ones[:, :], row_b[:, 0:D], start=False,
                                              stop=True)
                    mm.then_inc(s_proj, 1)
                    mm_read = [(s_hn, b) if j < LAST else (s_hn_act, n)]
                if stage == "x_norm_turn":
                    wait_for(turn_read)
                    for i in range(n):
                        pe.wait_ge(*((s_xn_act, j) if i else (s_xn, j + 1)))
                        mm = nc.tensor.transpose(turn_ps[:, i * D:(i + 1) * D], xn[:, a + i, :], ident[:, :])
                    mm.then_inc(s_xnT_ps, 1)
                    turn_read = [(s_xnT2, j + 1)]
                if stage == "down":
                    wait_for(kv_read)
                    if j == 0:
                        pe.wait_ge(s_wa, 16)
                    pe.wait_ge(s_xnT, j + 1)
                    for i in range(n):
                        mm = nc.tensor.matmul(kv_ps[:, i * LATENT:(i + 1) * LATENT], xnT[:, a + i, :],
                                              w_a[:, WDOWN:WDOWN + LATENT], start=True, stop=True)
                    mm.then_inc(s_down, 1)
                    kv_read = [(s_cn, 2 * b) if j < LAST else (s_cn_act, 2 * n)]
                if stage == "down_turn":
                    wait_for(turn_read)
                    for i in range(n):
                        pe.wait_ge(*((s_cn, 2 * (a + i) + 1) if j < LAST else (s_cn_act, 2 * i + 1)))
                        nc.tensor.transpose(turn_ps[0:DQ, i * D:(i + 1) * D], cn[:, a + i, 0:DQ], ident[:, :])
                        pe.wait_ge(*((s_cn, 2 * (a + i) + 2) if j < LAST else (s_cn_act, 2 * i + 2)))
                        mm = nc.tensor.transpose(turn_ps[0:DKV, (n + i) * D:(n + i + 1) * D], cn[:, a + i, DQ:],
                                                 ident[:, :])
                    mm.then_inc(s_cT_ps, 1)
                    turn_read = [(s_ckvT, j + 1)]
                if stage == "up_q":
                    wait_for(mm_read)
                    pe.wait_ge(s_xnT2, j + 1)
                    for i in range(n):
                        for par in range(2):
                            at = i * UPQ + D + (1 + par) * HEADS * R
                            nc.tensor.matmul(mm_ps[:, at:at + HEADS * R], xnT2[:, a + i, par, :],
                                             w_a[:, WKR:WKR + HEADS * R], start=True, stop=True)
                    pe.wait_ge(s_cqT, j + 1)
                    for i in range(n):
                        mm = nc.tensor.matmul(mm_ps[:, i * UPQ:i * UPQ + D + HEADS * R], cqT[:, a + i, :],
                                              w_q[:, 0:D + HEADS * R], start=True, stop=True)
                    mm.then_inc(s_up_q, 1)
                    mm_read = [(s_rot, j + 1), (s_q_plain, b)]
                if stage == "up_kv":
                    wait_for(kv_read)
                    pe.wait_ge(s_ckvT, [g for g, ts in enumerate(GROUPS) if j in ts][0] + 1)
                    for par in range(2):
                        mm = nc.tensor.matmul(kv_ps[:, par * 2 * D:(par + 1) * 2 * D], ckvT[:, j, par, :],
                                              w_kv[:, 0:2 * D], start=True, stop=True)
                    mm.then_inc(s_up_kv, 1)
                    kv_read = [(s_k, j + 1), (s_v, j + 1)]
                if stage == "mix_turn":
                    wait_for(turn_read)
                    pe.wait_ge(s_on, j + 1)
                    nc.tensor.transpose(turn_ps[:, 0:D], on[:, j, :], ident[:, :]).then_inc(s_onT_ps, 1)
                    turn_read = [(s_onT, j + 1)]
                if stage == "attn_out":
                    wait_for(kv_read)
                    nc.tensor.matmul(kv_ps[:, 0:D], ident[:, :], h1[:, j, :], start=True, stop=False)
                    pe.wait_ge(s_onT, j + 1)
                    nc.tensor.matmul(kv_ps[:, 0:D], onT[:, j, :], w_a[:, WOUT:WOUT + D], start=False, stop=True) \
                        .then_inc(s_h2_ps, 1)
                    kv_read = [(s_xg, j + 1), (s_h2h, j + 1)]
                if stage == "gru_in_turn":
                    wait_for(turn_read)
                    pe.wait_ge(s_xg, j + 1)
                    nc.tensor.transpose(turn_ps[:, 0:D], xg[:, j, :], ident[:, :]).then_inc(s_xgT_ps, 1)
                    turn_read = [(s_xgT, j + 1)]
                if stage == "gru_x":
                    if j == 0:
                        pe.wait_ge(s_wg, 16)
                    pe.wait_ge(s_xgT, j + 1)
                if stage in ("gru_x", "gru_x_update", "gru_x_candidate"):
                    both = xgT[:, 2 * j:2 * j + 2, :].rearrange("p s b -> p (s b)")
                if stage == "gru_x":
                    for m in range(KC):
                        if j:
                            pe.wait_ge(s_tr[m], 2 * j - 1)
                        nc.tensor.matmul(r_ps[m][:, 0:2 * B], w_x(RG, m), both, start=True, stop=False,
                                         skip_group_check=True)
                if stage == "gru_x_update":
                    for m in range(KC):
                        if j:
                            pe.wait_ge(s_tz[m], 2 * j)
                        mm = nc.tensor.matmul(z_ps[:, 2 * m * B:(2 * m + 2) * B], w_x(ZG, m), both, start=(m == 0),
                                              stop=(j == 0), skip_group_check=True)
                    if j == 0:
                        mm.then_inc(s_z_ps, 1)
                if stage == "gru_x_candidate":
                    for m in range(KC):
                        if j:
                            pe.wait_ge(s_tc[m], 2 * j)
                        mm = nc.tensor.matmul(c_ps[m][:, 0:2 * B], w_x(CG, m), both, start=True, stop=(j == 0),
                                              skip_group_check=True)
                        if j == 0:
                            mm.then_inc(s_c_ps[m], 1)
                t = j
                if stage == "gru_reset" and t:
                    if t == 1:
                        pe.wait_ge(s_scaled, 1)
                    for kc in range(KC):
                        pe.wait_ge(s_hs[kc], t)
                        for m in range(KC):
                            mm = nc.tensor.matmul(r_cols(m, t), w_h(RG, kc, m), hs[:, kc, t - 1, :], start=False,
                                                  stop=(kc == KC - 1), skip_group_check=True)
                            if kc == KC - 1:
                                mm.then_inc(s_r_ps[m], 1)
                if stage == "gru_update":
                    for m in range(KC) if t else ():
                        for kc in range(KC):
                            mm = nc.tensor.matmul(z_cols(m, t), w_h(ZG, kc, m), hs[:, kc, t - 1, :],
                                                  start=False, stop=(kc == KC - 1), skip_group_check=True)
                    if t:
                        mm.then_inc(s_z_ps, 1)
                if stage == "gru_candidate" and t:
                    if t == 1:
                        pe.wait_ge(s_scaled, 2)
                    for kc in range(KC):
                        pe.wait_ge(s_rh[kc], t)
                        for m in range(KC):
                            mm = nc.tensor.matmul(c_cols(m, t), w_h(CG, kc, m), rh[:, kc, :], start=False,
                                                  stop=(kc == KC - 1), skip_group_check=True)
                            if kc == KC - 1:
                                mm.then_inc(s_c_ps[m], 1)
                if stage == "gru_candidate" and t < T - 1:
                    if t:
                        pe.wait_ge(s_tr[0], t)
                    for _ in range(FILL[t]):
                        nc.tensor.matmul(r_ps[0][:, 2 * B:6 * B], zeros[:, 0:128], zeros[:, 0:4 * B],
                                         start=False, stop=False, skip_group_check=True)
                if stage == "out_first":
                    wait_for(mm_read)
                    nc.tensor.matmul(mm_ps[0:B, 0:D], ones[:, 0:B], row_b[:, D:2 * D], start=True, stop=False)
                    for kc in range(KC):
                        pe.wait_ge(s_hs[kc], 2 * j + 1)
                        mm = nc.tensor.matmul(mm_ps[0:B, 0:D], hs[:, kc, 2 * j, :], w_o(kc), start=False,
                                              stop=(kc == KC - 1))
                    mm.then_inc(s_out_ps, 1)
                    mm_read = [(s_ot, NT)]
                if stage == "out":
                    wait_for(mm_read)
                    nc.tensor.matmul(mm_ps[:, 0:D], ones[:, :], row_b[:, D:2 * D], start=True, stop=False)
                    if j == 0:
                        pe.wait_ge(s_scaled, 3)
                    for kc in range(KC):
                        pe.wait_ge(s_hs[kc], 2 * j + 2)
                        both = hs[:, kc, 2 * j:2 * j + 2, :].rearrange("p s b -> p (s b)")
                        mm = nc.tensor.matmul(mm_ps[:, 0:D], both, w_o(kc), start=False, stop=(kc == KC - 1))
                    mm.then_inc(s_out_ps, 1)
                    mm_read = [(s_ot, j + 1)]


def kernel(**inputs):
    import concourse.bacc as bacc
    from concourse.bass_utils import run_bass_kernel_spmd

    a = {n: np.asarray(w) for n, w in inputs.items()}

    def chunks(w):
        return w.reshape(-1, 128, w.shape[1]).transpose(1, 0, 2).reshape(128, -1)

    f, g = "L0_attn_", "L0_ffn_"
    pack_a = np.concatenate([chunks(a["L0_tok_W"]), a[f + "W_dq"], a[f + "W_dkv"], a[f + "W_kr"], a[f + "W_o"].T], 1)
    pack_q = np.concatenate([a[f + "W_uq"], a[f + "W_qr"], a[f + "q_ln_g"][:, None],
                             a[f + "q_ln_b"][:, None]], 1)
    pack_kv = np.concatenate([a[f + "W_ukv"], a[f + "kv_ln_g"][:, None], a[f + "kv_ln_b"][:, None]], 1)
    rows = np.stack([np.concatenate([a["L0_tok_b"], a[g + "bo"]]),
                     np.concatenate([a["L0_tok_gamma"], a["L0_tok_beta"]])])
    pack_g = np.concatenate([a[g + n].T for n in ("Wur", "Wuz", "Wu")] +
                            [chunks(a[g + n].T) for n in ("Wwr", "Wwz", "Ww", "Wo")] +
                            [chunks(a[g + n][:, None]) for n in ("bur", "buz", "bu", "bwr", "bwz", "bw")], 1)
    time = np.arange(T, dtype=np.float32)
    cos = np.repeat(np.cos(time)[:, None], HEADS * R, 1)
    sin = np.sin(time)[:, None] * np.tile(np.array([-1, 1], np.float32), HEADS)
    rot = np.stack([cos, sin], 1).reshape(NT, 2, 2, HEADS * R).astype(np.float32)
    query = np.repeat(rot.transpose(1, 0, 2, 3), B, 0)[:, :, :, None]
    keys = np.broadcast_to(rot.transpose(0, 2, 1, 3)[None], (128, NT, 2, 2, HEADS * R))
    rope = np.concatenate([query, keys], 3).reshape(128, NT, 2, ROT)
    arrays = {"x": a["x"].reshape(B, -1), "pack_a": pack_a, "pack_q": pack_q, "pack_kv": pack_kv, "rows": rows,
              "pack_g": pack_g, "rope": rope}
    arrays = {n: np.ascontiguousarray(w) for n, w in arrays.items()}
    nc = bacc.Bacc("TRN2", target_bir_lowering=False, num_devices=1)
    args = [nc.dram_tensor(n, w.shape, mybir.dt.from_np(w.dtype), kind="ExternalInput").ap() for n, w in arrays.items()]
    out = nc.dram_tensor("out", (B, T, D), F32, kind="ExternalOutput").ap()
    audio_tower(nc, *args, out)
    r = run_bass_kernel_spmd(nc, [arrays], core_ids=[0])
    return r.results[0]["out"]
```
